# Optimizing a Trainium2 kernel written in Bass

```python
import numpy as np
import jax
import jax.numpy as jnp

def _softmax(x, axis=-1):
    return jax.nn.softmax(x, axis=axis)
def _gelu(x):
    return jax.nn.gelu(x, approximate=True)
def _silu(x):
    return jax.nn.silu(x)
def _sigmoid(x):
    return jax.nn.sigmoid(x)
def _layernorm(x, axis=-1, eps=1e-5):
    m = jnp.mean(x, axis=axis, keepdims=True)
    v = jnp.var(x, axis=axis, keepdims=True)
    return (x - m) / jnp.sqrt(v + eps)
def _scatter_add(tgt, idx, src, axis=0):
    return tgt.at[idx].add(src)
def _segment_sum(src, seg, n):
    return jax.ops.segment_sum(src, seg, n)

kernel_name = 'mk_conv_preact_d2_conv_nhwc96_bfefe8'

def setup_inputs(seed: int = 0):
    np.random.seed(seed)
    _w = jnp.asarray
    def _rec_inputs():
        import jax
        import jax.numpy as jnp
        _gk = jax.random.key(seed)
        x = -0.0005963 + 1.001 * jax.random.normal(jax.random.fold_in(_gk, 1), (8, 64, 64, 96), jnp.float32)
        return x
    x = _rec_inputs()
    def _L0_conv_setup():
        import jax, jax.numpy as jnp
        import numpy as np
        from jax import lax
        D_MODEL, D_INNER, D_STATE, DT_RANK, K = (96, 192, 16, 6, 4)
        B_, H_, W_ = (8, 64, 64)

        def _selective_scan(xs, delta, A, Bs, Cs, Dk):
            u_t = xs.transpose(3, 0, 1, 2)
            d_t = delta.transpose(3, 0, 1, 2)
            B_t = Bs.transpose(3, 0, 1, 2)
            C_t = Cs.transpose(3, 0, 1, 2)
            b = xs.shape[0]
            h0 = jnp.zeros((b, K, D_INNER, D_STATE), xs.dtype)

            def step(h, inp):
                ul, dl, Bl, Cl = inp
                dA = jnp.exp(dl[..., None] * A)
                h = dA * h + (dl * ul)[..., None] * Bl[:, :, None, :]
                y = jnp.einsum('bkdn,bkn->bkd', h, Cl)
                return (h, y)
            _, ys = lax.scan(step, h0, (u_t, d_t, B_t, C_t))
            y = ys.transpose(1, 2, 3, 0)
            return y + xs * Dk[None, :, :, None]
        key = jax.random.key(seed)
        ks = jax.random.split(key, 12)
        return {'x': jax.random.normal(ks[0], (B_, H_, W_, D_MODEL), jnp.float32), 'in_proj_w': jax.random.normal(ks[1], (2 * D_INNER, D_MODEL), jnp.float32) * 0.05, 'conv_w': jax.random.normal(ks[2], (D_INNER, 1, 3, 3), jnp.float32) * 0.1, 'conv_b': jax.random.normal(ks[3], (D_INNER,), jnp.float32) * 0.01, 'x_proj_w': jax.random.normal(ks[4], (K, DT_RANK + 2 * D_STATE, D_INNER), jnp.float32) * 0.05, 'dt_proj_w': jax.random.normal(ks[5], (K, D_INNER, DT_RANK), jnp.float32) * 0.1, 'dt_proj_b': jax.random.normal(ks[6], (K, D_INNER), jnp.float32) * 0.1, 'A_logs': jax.random.uniform(ks[7], (K * D_INNER, D_STATE), jnp.float32, 0.0, 2.0), 'Ds': jnp.ones((K * D_INNER,), jnp.float32), 'ln_g': jnp.ones((D_INNER,), jnp.float32), 'ln_b': jnp.zeros((D_INNER,), jnp.float32), 'out_proj_w': jax.random.normal(ks[8], (D_MODEL, D_INNER), jnp.float32) * 0.05}
    _L0_conv_all = _L0_conv_setup()
    _L0_conv_in = {k: v for k, v in _L0_conv_all.items() if k in ('in_proj_w', 'conv_w', 'conv_b', 'x_proj_w', 'dt_proj_w', 'dt_proj_b', 'A_logs', 'Ds', 'ln_g', 'ln_b', 'out_proj_w', )}
    del _L0_conv_all

    def _L1_conv_setup():
        import jax, jax.numpy as jnp
        import numpy as np
        UP = 2

        def _rect_1d(N, cutoff, edge_val):
            lo = int(N * cutoff // 2)
            hi = int(N - lo)
            r = np.ones(N, dtype=np.float32)
            r[lo + 1:hi] = 0.0
            if cutoff * N % 2 == 0:
                r[lo] = edge_val
                r[hi] = edge_val
            return r

        def _rect_mask_rfft(N, cutoff, edge_val):
            r = _rect_1d(N, cutoff, edge_val)
            m = r[:, None] * r[None, :]
            return jnp.asarray(m[:, :N // 2 + 1])

        def _upsample_rfft(x):
            B, C, H, W = x.shape
            z = jnp.zeros((B, C, H, UP, W, UP), x.dtype)
            z = z.at[:, :, :, 0, :, 0].set(x)
            xu = z.reshape(B, C, H * UP, W * UP)
            mask = _rect_mask_rfft(W * UP, 1.0 / UP, 1.0)
            xf = jnp.fft.rfft2(xu) * (UP * UP) * mask
            return jnp.fft.irfft2(xf, s=(H * UP, W * UP)).astype(x.dtype)

        def _lpf_rfft(x, cutoff=0.5):
            H, W = (x.shape[-2], x.shape[-1])
            mask = _rect_mask_rfft(W, cutoff, 0.5)
            xf = jnp.fft.rfft2(x) * mask
            return jnp.fft.irfft2(xf, s=(H, W)).astype(x.dtype)
        key = jax.random.key(seed)
        ks = jax.random.split(key, 6)
        B, H, W, dim = (16, 64, 64, 96)
        hidden = 4 * dim
        x = jax.random.normal(ks[0], (B, H, W, dim), jnp.float32)
        W1 = jax.random.normal(ks[1], (hidden, dim), jnp.float32) * 0.02
        b1 = jnp.zeros((hidden,), jnp.float32)
        W2 = jax.random.normal(ks[2], (dim, hidden), jnp.float32) * 0.02
        b2 = jnp.zeros((dim,), jnp.float32)
        init_coef = jnp.asarray([0.0169394634313126, 0.5, 0.3078363963999393], jnp.float32)
        coef = jnp.tile(init_coef[None, :], (hidden, 1))
        return {'x': x, 'W1': W1, 'b1': b1, 'W2': W2, 'b2': b2, 'coef': coef}
    _L1_conv_all = _L1_conv_setup()
    _L1_conv_in = {k: v for k, v in _L1_conv_all.items() if k in ('W1', 'b1', 'W2', 'b2', 'coef', )}
    del _L1_conv_all

    return {
        "x": x,
        "L0_conv_in_proj_w": _L0_conv_in["in_proj_w"],
        "L0_conv_conv_w": _L0_conv_in["conv_w"],
        "L0_conv_conv_b": _L0_conv_in["conv_b"],
        "L0_conv_x_proj_w": _L0_conv_in["x_proj_w"],
        "L0_conv_dt_proj_w": _L0_conv_in["dt_proj_w"],
        "L0_conv_dt_proj_b": _L0_conv_in["dt_proj_b"],
        "L0_conv_A_logs": _L0_conv_in["A_logs"],
        "L0_conv_Ds": _L0_conv_in["Ds"],
        "L0_conv_ln_g": _L0_conv_in["ln_g"],
        "L0_conv_ln_b": _L0_conv_in["ln_b"],
        "L0_conv_out_proj_w": _L0_conv_in["out_proj_w"],
        "L1_conv_W1": _L1_conv_in["W1"],
        "L1_conv_b1": _L1_conv_in["b1"],
        "L1_conv_W2": _L1_conv_in["W2"],
        "L1_conv_b2": _L1_conv_in["b2"],
        "L1_conv_coef": _L1_conv_in["coef"],
    }

def reference(x, L0_conv_in_proj_w, L0_conv_conv_w, L0_conv_conv_b, L0_conv_x_proj_w, L0_conv_dt_proj_w, L0_conv_dt_proj_b, L0_conv_A_logs, L0_conv_Ds, L0_conv_ln_g, L0_conv_ln_b, L0_conv_out_proj_w, L1_conv_W1, L1_conv_b1, L1_conv_W2, L1_conv_b2, L1_conv_coef):
    import jax
    import jax.numpy as jnp
    def _L0_conv_ref(x, in_proj_w, conv_w, conv_b, x_proj_w, dt_proj_w, dt_proj_b, A_logs, Ds, ln_g, ln_b, out_proj_w):
        import jax, jax.numpy as jnp
        import numpy as np
        from jax import lax
        D_MODEL, D_INNER, D_STATE, DT_RANK, K = (96, 192, 16, 6, 4)
        B_, H_, W_ = (8, 64, 64)

        def _selective_scan(xs, delta, A, Bs, Cs, Dk):
            u_t = xs.transpose(3, 0, 1, 2)
            d_t = delta.transpose(3, 0, 1, 2)
            B_t = Bs.transpose(3, 0, 1, 2)
            C_t = Cs.transpose(3, 0, 1, 2)
            b = xs.shape[0]
            h0 = jnp.zeros((b, K, D_INNER, D_STATE), xs.dtype)

            def step(h, inp):
                ul, dl, Bl, Cl = inp
                dA = jnp.exp(dl[..., None] * A)
                h = dA * h + (dl * ul)[..., None] * Bl[:, :, None, :]
                y = jnp.einsum('bkdn,bkn->bkd', h, Cl)
                return (h, y)
            _, ys = lax.scan(step, h0, (u_t, d_t, B_t, C_t))
            y = ys.transpose(1, 2, 3, 0)
            return y + xs * Dk[None, :, :, None]
        B, H, W, C = x.shape
        L = H * W
        xz = jnp.einsum('bhwc,ec->bhwe', x, in_proj_w)
        xc, z = jnp.split(xz, 2, axis=-1)
        xc = xc.transpose(0, 3, 1, 2)
        xc = lax.conv_general_dilated(xc, conv_w, (1, 1), 'SAME', dimension_numbers=('NCHW', 'OIHW', 'NCHW'), feature_group_count=D_INNER)
        xa = jax.nn.silu(xc + conv_b[None, :, None, None])
        x_flat = xa.reshape(B, D_INNER, L)
        x_wh = xa.transpose(0, 1, 3, 2).reshape(B, D_INNER, L)
        x_hwwh = jnp.stack([x_flat, x_wh], axis=1)
        xs = jnp.concatenate([x_hwwh, jnp.flip(x_hwwh, -1)], axis=1)
        x_dbl = jnp.einsum('bkdl,kcd->bkcl', xs, x_proj_w)
        dts = x_dbl[:, :, :DT_RANK]
        Bs = x_dbl[:, :, DT_RANK:DT_RANK + D_STATE]
        Cs = x_dbl[:, :, DT_RANK + D_STATE:]
        dts = jnp.einsum('bkrl,kdr->bkdl', dts, dt_proj_w)
        delta = jax.nn.softplus(dts + dt_proj_b[None, :, :, None])
        A = -jnp.exp(A_logs).reshape(K, D_INNER, D_STATE)
        Dk = Ds.reshape(K, D_INNER)
        out_y = _selective_scan(xs, delta, A, Bs, Cs, Dk)
        y1 = out_y[:, 0]
        inv = jnp.flip(out_y[:, 2:4], -1)
        y2 = inv[:, 0]
        y3 = out_y[:, 1].reshape(B, D_INNER, W, H).transpose(0, 1, 3, 2).reshape(B, D_INNER, L)
        y4 = inv[:, 1].reshape(B, D_INNER, W, H).transpose(0, 1, 3, 2).reshape(B, D_INNER, L)
        y = (y1 + y2 + y3 + y4).transpose(0, 2, 1).reshape(B, H, W, D_INNER)
        mu = y.mean(-1, keepdims=True)
        var = ((y - mu) ** 2).mean(-1, keepdims=True)
        y = (y - mu) * lax.rsqrt(var + 1e-05) * ln_g + ln_b
        y = y * jax.nn.silu(z)
        return jnp.einsum('bhwd,cd->bhwc', y, out_proj_w)

    def _L1_conv_ref(x, W1, b1, W2, b2, coef):
        import jax, jax.numpy as jnp
        import numpy as np
        UP = 2

        def _rect_1d(N, cutoff, edge_val):
            lo = int(N * cutoff // 2)
            hi = int(N - lo)
            r = np.ones(N, dtype=np.float32)
            r[lo + 1:hi] = 0.0
            if cutoff * N % 2 == 0:
                r[lo] = edge_val
                r[hi] = edge_val
            return r

        def _rect_mask_rfft(N, cutoff, edge_val):
            r = _rect_1d(N, cutoff, edge_val)
            m = r[:, None] * r[None, :]
            return jnp.asarray(m[:, :N // 2 + 1])

        def _upsample_rfft(x):
            B, C, H, W = x.shape
            z = jnp.zeros((B, C, H, UP, W, UP), x.dtype)
            z = z.at[:, :, :, 0, :, 0].set(x)
            xu = z.reshape(B, C, H * UP, W * UP)
            mask = _rect_mask_rfft(W * UP, 1.0 / UP, 1.0)
            xf = jnp.fft.rfft2(xu) * (UP * UP) * mask
            return jnp.fft.irfft2(xf, s=(H * UP, W * UP)).astype(x.dtype)

        def _lpf_rfft(x, cutoff=0.5):
            H, W = (x.shape[-2], x.shape[-1])
            mask = _rect_mask_rfft(W, cutoff, 0.5)
            xf = jnp.fft.rfft2(x) * mask
            return jnp.fft.irfft2(xf, s=(H, W)).astype(x.dtype)
        xc = jnp.transpose(x, (0, 3, 1, 2))
        xu = _upsample_rfft(xc)
        h = jnp.transpose(xu, (0, 2, 3, 1))
        h = h @ W1.T + b1
        h = coef[:, 0] + coef[:, 1] * h + coef[:, 2] * (h * h)
        h = h @ W2.T + b2
        hc = jnp.transpose(h, (0, 3, 1, 2))
        hl = _lpf_rfft(hc, cutoff=0.5)
        out = hl[:, :, ::2, ::2]
        return jnp.transpose(out, (0, 2, 3, 1))

    def _gn(v, G=32, eps=1e-5):
        B_, H_, W_, C_ = v.shape
        g = v.reshape(B_, H_, W_, G, C_ // G)
        m = jnp.mean(g, axis=(1, 2, 4), keepdims=True)
        s = jnp.var(g, axis=(1, 2, 4), keepdims=True)
        return ((g - m) / jnp.sqrt(s + eps)).reshape(v.shape)

    def _ln_c(v, eps=1e-6):
        m = jnp.mean(v, axis=-1, keepdims=True)
        s = jnp.var(v, axis=-1, keepdims=True)
        return (v - m) / jnp.sqrt(s + eps)

    def _ln_t(v, eps=1e-5):
        m = jnp.mean(v, axis=-1, keepdims=True)
        s = jnp.var(v, axis=-1, keepdims=True)
        return (v - m) / jnp.sqrt(s + eps)

    def _to_tokens(v):
        B_, H_, W_, C_ = v.shape
        return v.reshape(B_, H_ * W_, C_)
    def _from_tokens(t, like):
        return t.reshape(like.shape)

    x = x + _L0_conv_ref(_gn(x), L0_conv_in_proj_w, L0_conv_conv_w, L0_conv_conv_b, L0_conv_x_proj_w, L0_conv_dt_proj_w, L0_conv_dt_proj_b, L0_conv_A_logs, L0_conv_Ds, L0_conv_ln_g, L0_conv_ln_b, L0_conv_out_proj_w)
    x = x + _L1_conv_ref(_gn(x), L1_conv_W1, L1_conv_b1, L1_conv_W2, L1_conv_b2, L1_conv_coef)
    return x


_drawn_inputs = setup_inputs


def setup_inputs(seed=0):
    import zlib

    import numpy as np

    out = dict(_drawn_inputs(seed))
    spreads = {'L0_conv_Ds': (1.0, 0.6),
     'L0_conv_ln_g': (1.0, 0.2),
     'L0_conv_ln_b': (0.0, 0.49),
     'L1_conv_b1': (0.0, 0.446),
     'L1_conv_b2': (0.0, 0.1)}
    factors = {'L0_conv_conv_b': 4.517,
     'L0_conv_x_proj_w': 8.0,
     'L0_conv_dt_proj_w': 8.0,
     'L0_conv_dt_proj_b': 8.0,
     'L0_conv_A_logs': 8.0}
    for name, (base, spread) in spreads.items():
        noise = np.random.default_rng([zlib.crc32(name.encode()), seed]).standard_normal(out[name].shape)
        drawn = base * np.exp(spread * noise) if base else spread * noise
        out[name] = jnp.asarray(drawn.astype(out[name].dtype))
    for name, factor in factors.items():
        out[name] = (out[name] * factor).astype(out[name].dtype)
    return out
```

```python
from contextlib import ExitStack

import numpy as np

import concourse.bass as bass
from concourse import mybir

ALU = mybir.AluOpType
ACT = mybir.ActivationFunctionType
AX = mybir.AxisListType
F32 = mybir.dt.float32
F32R = mybir.dt.float32r

NB = 8
HW = 64
L = HW * HW
C = 96
ND = 192
NS = 16
NK = 4
NR = 6
HID = 384
PADW = HW + 2
TC = 1024
NCH = L // TC
NG = 4
NJ = 3


class Queue:

    def __init__(self, sem):
        self.sem = sem
        self.n = 0
        self.items = []
        self.waited = {}

    def wait(self, *marks):
        for m in marks:
            if m is None:
                continue
            sem, count = m
            if self.waited.get(sem.num, 0) < count:
                self.waited[sem.num] = count
                self.items.append((0, sem, count))

    def op(self, fn, *marks):
        self.wait(*marks)
        self.n += 1
        self.items.append((1, fn, self.sem, 1))
        return (self.sem, self.n)

    def emit(self, eng):
        for it in self.items:
            if it[0] == 0:
                eng.wait_ge(it[1], it[2])
            elif it[0] == 2:
                eng.preload_act_table_set("natural_log_exp_and_others")
            else:
                it[1](eng).then_inc(it[2], it[3])


class DmaRing:

    def __init__(self, queue, sems):
        self.queue = queue
        self.sems = sems
        self.counts = [0] * len(sems)
        self.i = 0

    def dma(self, out, in_, *marks):
        k = self.i % len(self.sems)
        self.i += 1
        if self.counts[k]:
            self.queue.wait((self.sems[k], self.counts[k]))
        self.queue.wait(*marks)
        self.counts[k] += 16
        self.queue.items.append((1, lambda e: e.dma_start(out, in_), self.sems[k], 16))
        return (self.sems[k], self.counts[k])

    def drain(self):
        for s, c in zip(self.sems, self.counts):
            if c:
                self.queue.wait((s, c))


class Phase:

    def __init__(self, nc, ctx, name):
        def sem(x):
            return ctx.enter_context(nc.semaphore(f"{name}_{x}"))

        self.nc = nc
        self.pe, self.ve, self.ac, self.po, self.sp = (Queue(sem(x)) for x in ("pe", "ve", "ac", "po", "sp"))
        self.ld = DmaRing(self.sp, [sem(f"ld{i}") for i in range(6)])
        self.st = DmaRing(self.sp, [sem(f"st{i}") for i in range(6)])

    def run(self):
        self.ld.drain()
        self.st.drain()
        with self.nc.Block() as block:
            @block.sync
            def _(e):
                self.sp.emit(e)

            @block.tensor
            def _(e):
                self.pe.emit(e)

            @block.vector
            def _(e):
                self.ve.emit(e)

            @block.scalar
            def _(e):
                self.ac.emit(e)

            @block.gpsimd
            def _(e):
                self.po.emit(e)


def pre_phase(nc, P, T, S):
    win, cwr, cb, gmat, eps = (T(n, s) for n, s in (
        ("win", [C, 2 * ND]), ("cwr", [C, 9, ND]), ("cb", [C, 2]), ("gmat", [C, C]), ("eps", [C, 1])))
    wtap = T("wtap", [C, 9, ND])
    m_w = [P.ld.dma(win[:], S["winT"]), P.ld.dma(cwr[:], S["cwr"]), P.ld.dma(cb[:], S["cb"]),
           P.ld.dma(gmat[:], S["gmat"])]
    m_eps = P.ve.op(lambda e: e.memset(eps[:], 1e-5))
    m_tap = None
    for t in range(9):
        m_tap = P.ve.op(lambda e, t=t: e.tensor_tensor(wtap[:, t, :], win[:, 0:ND], cwr[:, t, :], ALU.mult), *m_w)

    xt = [T(f"xt{i}", [C, L]) for i in range(2)]
    xp = [T(f"xp{i}", [C, PADW, PADW]) for i in range(2)]
    xs = [T(f"xs{i}", [C, 2048]) for i in range(4)]
    st = T("st", [C, 8, 6])
    mv = T("mv", [C, 8])
    ps = S["psum"]
    m_pad = [P.po.op(lambda e, i=i: e.memset(xp[i][:], 0.0)) for i in range(2)]
    xt_free = [None, None]
    xp_free = [None, None]
    ps_free = [None] * 8
    xs_free = [None] * 4
    mv_free = None
    pi = xi = 0
    for b in range(NB):
        s = b % 2
        m_x = P.ld.dma(xt[s][:], S["xT"][b], xt_free[s])
        for i in range(8):
            m = P.ve.op(lambda e, i=i, s=s: e.bn_stats(st[:, i, :], xt[s][:, i * 512:(i + 1) * 512]), m_x)
        m = P.ve.op(lambda e: e.bn_aggr(mv[:, 0:2], st[:].rearrange("p a b -> p (a b)")), m, mv_free)
        m = P.ve.op(lambda e: e.scalar_tensor_tensor(mv[:, 1:2], mv[:, 0:1], mv[:, 0:1], mv[:, 1:2], ALU.mult, ALU.add), m)
        g = pi % 8
        pi += 1
        m = P.pe.op(lambda e, g=g: e.matmul(ps[g][0:C, 0:2], gmat[:], mv[:, 0:2], start=True, stop=True),
                    m, m_w[3], ps_free[g])
        m = ps_free[g] = P.ve.op(lambda e, g=g: e.tensor_copy(mv[:, 2:4], ps[g][0:C, 0:2]), m)
        m = P.ve.op(lambda e: e.scalar_tensor_tensor(mv[:, 4:5], mv[:, 2:3], mv[:, 2:3], mv[:, 3:4], ALU.mult, ALU.subtract), m)
        m = P.ac.op(lambda e: e.activation(mv[:, 5:6], mv[:, 4:5], ACT.Ln, bias=eps[:], scale=-1.0), m, m_eps)
        m = P.ac.op(lambda e: e.activation(mv[:, 6:7], mv[:, 5:6], ACT.Exp, scale=-0.5), m)
        m = P.ve.op(lambda e: e.scalar_tensor_tensor(mv[:, 7:8], mv[:, 2:3], -1.0, mv[:, 6:7], ALU.mult, ALU.mult), m)
        m_n = P.ac.op(lambda e, s=s: e.activation(
            xp[s][:, 1:HW + 1, 1:HW + 1], xt[s][:].rearrange("p (h w) -> p h w", w=HW),
            ACT.Identity, bias=mv[:, 7:8], scale=mv[:, 6:7]), m, m_pad[s], xp_free[s])
        xt_free[s] = m_n
        mv_free = m_n
        for q in range(2):
            for kind in range(2):
                for half in range(2):
                    x = xi % 4
                    xi += 1
                    for r in range(4):
                        h0 = (q * 4 + r) * 8
                        g = pi % 8
                        pi += 1

                        def mm(e, g=g, s=s, h0=h0, half=half, kind=kind):
                            if kind == 1:
                                return e.matmul(ps[g][0:C, :], win[:, ND + half * C:ND + (half + 1) * C],
                                                xp[s][:, h0 + 1:h0 + 9, 1:HW + 1], start=True, stop=True)
                            for t in range(9):
                                i = e.matmul(ps[g][0:C, :], wtap[:, t, half * C:(half + 1) * C],
                                             xp[s][:, h0 + t // 3:h0 + t // 3 + 8, t % 3:t % 3 + HW],
                                             start=(t == 0), stop=(t == 8))
                            return i
                        m = P.pe.op(mm, m_n, m_tap, ps_free[g])
                        if r == 0:
                            P.ac.wait(xs_free[x])
                        bias = cb[:, half:half + 1] if kind == 0 else 0.0
                        m = ps_free[g] = P.ac.op(lambda e, g=g, x=x, r=r, bias=bias: e.activation(
                            xs[x][:, r * 512:(r + 1) * 512], ps[g][0:C, :], ACT.Silu, bias=bias), m, *m_w)
                        last_pe = (P.pe.sem, P.pe.n)
                    dst = S["xa"] if kind == 0 else S["sz"]
                    xs_free[x] = P.st.dma(dst[b, half, :, q * 2048:(q + 1) * 2048], xs[x][:], m)
        xp_free[s] = last_pe
    P.run()


def scan_phase(nc, P, T, S):
    wx = T("wx", [C, NK, 2, C])
    dtw = T("dtw", [38, NK * ND])
    dtb = T("dtb", [C, NK * 2])
    ndtb = T("ndtb", [C, NK * 2])
    ds = T("ds", [C, 2, NK])
    dsum = T("dsum", [C, 2])
    c20 = T("c20", [C, 1])
    am = T("am", [128, NK * 2 * NJ * NG])
    selbf = T("selbf", [C, 8, 128])
    selb = T("selb", [C, 8, 128], F32R)
    seld = T("seld", [C, NJ, 128])
    sely = T("sely", [128, 32])
    m_c = [P.ld.dma(wx[:], S["wx"]), P.ld.dma(dtw[32:38, :], S["dtw"]), P.ld.dma(dtb[:], S["dtb"]),
           P.ld.dma(ds[:], S["ds"]), P.ld.dma(am[:], S["alog"]), P.ld.dma(selbf[:], S["selb"]),
           P.ld.dma(seld[:], S["seld"]), P.ld.dma(sely[:], S["sely"])]
    P.ac.items.append((2,))
    m = P.ac.op(lambda e: e.activation(am[:], am[:], ACT.Exp), *m_c)
    m_am = P.ac.op(lambda e: e.mul(am[:], am[:], -1.0), m)
    m_sel = P.ve.op(lambda e: e.tensor_copy(selb[:], selbf[:]), *m_c)
    m_c20 = P.ve.op(lambda e: e.memset(c20[:], 20.0))
    m_nb = P.ve.op(lambda e: e.tensor_scalar(ndtb[:], dtb[:], -1.0, 20.0, ALU.mult, ALU.add))
    m_ds = P.ve.op(lambda e: e.tensor_reduce(dsum[:], ds[:], AX.X, ALU.add))

    u = T("u", [C, 2, L])
    ya = T("ya", [C, 2, L])
    rep = T("rep", [128, NG, 2, TC])
    NRING = 4
    dlr = T("dlr", [128, NRING, TC])
    dur = T("dur", [128, NRING, TC])
    NE, NH, NC_ = 3, 3, 4
    E = T("E", [128, NE, TC])
    H = T("H", [128, NH, TC])
    HC = T("HC", [128, NC_, TC])
    dl = T("dl", [C, TC])
    dlu = T("dlu", [C, TC])
    sx = T("sx", [C, TC], F32R)
    dts = T("dts", [38, TC])
    car = T("car", [128, 2 * NJ * NG])
    psum = S["psumall"]
    stage = [psum[:, 0:1024], psum[:, 1024:2048]]
    dbu = psum[:, 2048:3072]
    yps = psum[:, 3072:4096]

    free = {}
    stage_n = [0]

    def view(t, k, half, t0):
        if k % 2 == 0:
            return t[:, half, t0:t0 + TC]
        return t[:, half, :].rearrange("p (h w) -> p w h", w=HW)[:, t0 // HW:(t0 + TC) // HW, :]

    def viewn(t, k, half, t0, n):
        if k % 2 == 0:
            return t[:, half, t0:t0 + n]
        return t[:, half, :].rearrange("p (h w) -> p w h", w=HW)[:, t0 // HW:(t0 + n) // HW, :]

    def shaped(ap, k):
        return ap if k % 2 == 0 else ap.rearrange("p (w h) -> p w h", h=HW)

    def next_stage():
        i = stage_n[0] % 2
        stage_n[0] += 1
        return i, free.get(("stage", i))

    steps = [(b, k, ci, half) for b in range(NB) for k in range(NK) for ci in range(NCH) for half in range(2)]
    m_u = {}
    m_yinit = {}
    ring_n = [0]
    rep_ready = {}
    rep_used = {}
    slots = {}
    last_u_read = [None]
    u_reads = []

    def t_of(k, ci):
        return TC * (ci if k < 2 else NCH - 1 - ci)

    def load_u(b):
        m_u[b] = [P.ld.dma(u[:, h, :], S["xa"][b, h], *u_reads) for h in range(2)]

    def prep(n):
        b, k, ci, half = steps[n]
        t0 = t_of(k, ci)
        st = {}

        def xproj():
            i, fr = next_stage()

            def mm(e):
                for sub in range(2):
                    for h in range(2):
                        r = e.matmul(stage[i][0:C, sub * 512:(sub + 1) * 512], wx[:, k, h, :],
                                     viewn(u, k, h, t0 + sub * 512, 512), start=(h == 0), stop=(h == 1))
                return r
            m = P.pe.op(mm, fr, *m_u[b], *m_c)
            u_reads.append(m)
            md = P.ac.op(lambda e: e.copy(dts[32:38, :], stage[i][32:38, :]), m, free.get("dts"))
            ms = P.ac.op(lambda e: e.copy(sx[:], stage[i][0:C, :]), m, free.get("sx"))
            mv = P.ve.op(lambda e: e.tensor_tensor(sx[64:96, :], stage[i][64:96, :], sx[64:96, :], ALU.subtract), ms, md)
            free[("stage", i)] = mv
            st_sx[0] = mv
            st_dts[0] = md

        def reps(g):
            def f():
                for c in range(2):
                    i, fr = next_stage()

                    def mm(e, i=i, c=c):
                        for sub in range(2):
                            r = e.matmul(stage[i][:, sub * 512:(sub + 1) * 512], selb[:, 2 * g + c, :],
                                         sx[:, sub * 512:(sub + 1) * 512], start=True, stop=True)
                        return r
                    m = P.pe.op(mm, fr, st_sx[0], m_sel)
                    free["sx"] = m
                    mr = P.ac.op(lambda e, i=i, c=c: e.copy(rep[:, g, c, :], stage[i][:]), m,
                                 rep_used.get((g, c)))
                    free[("stage", i)] = mr
                    rep_ready[(g, c)] = mr
            return f

        def dt():
            i, fr = next_stage()

            def mm(e):
                for sub in range(2):
                    r = e.matmul(stage[i][0:C, sub * 512:(sub + 1) * 512],
                                 dtw[32:38, k * ND + half * C:k * ND + (half + 1) * C],
                                 dts[32:38, sub * 512:(sub + 1) * 512], start=True, stop=True)
                return r
            m = P.pe.op(mm, fr, st_dts[0], *m_c)
            free["dts"] = m
            kk = k * 2 + half
            m1 = P.ac.op(lambda e: e.activation(dlu[:], stage[i][0:C, :], ACT.Relu, bias=ndtb[:, kk:kk + 1], scale=-1.0),
                         m, free.get("dlu"), m_nb)
            m1 = P.ac.op(lambda e: e.activation(dlu[:], dlu[:], ACT.Exp, bias=c20[:], scale=-1.0), m1, m_c20)
            m1 = P.ac.op(lambda e: e.activation(dlu[:], dlu[:], ACT.Ln, bias=1.0), m1)
            st["ln"] = m1
            st["i"] = i

        def dlm():
            i = st["i"]
            kk = k * 2 + half
            m = P.ve.op(lambda e: e.scalar_tensor_tensor(dl[:], stage[i][0:C, :], dtb[:, kk:kk + 1], dlu[:], ALU.add, ALU.max),
                        st["ln"], free.get("dl"))
            free[("stage", i)] = m
            st["dl"] = m

        def dlum():
            m = P.po.op(lambda e: e.tensor_tensor(shaped(dlu[:], k), shaped(dl[:], k), view(u, k, half, t0), ALU.mult),
                        st["dl"], *m_u[b])
            u_reads.append(m)
            st["dlu"] = m

        def bc(j):
            def f():
                r = ring_n[0] % NRING
                ring_n[0] += 1
                slots[(n, j)] = r
                for (src, dst, key, mk) in ((dl, dlr, "dl", st["dl"]), (dlu, dur, "dlu", st["dlu"])):
                    i, fr = next_stage()

                    def mm(e, i=i, src=src):
                        for sub in range(2):
                            x = e.matmul(stage[i][:, sub * 512:(sub + 1) * 512], seld[:, j, :],
                                         src[:, sub * 512:(sub + 1) * 512], start=True, stop=True)
                        return x
                    m = P.pe.op(mm, fr, mk)
                    free[key] = m
                    ma = P.ac.op(lambda e, i=i, dst=dst: e.copy(dst[:, r, :], stage[i][:]), m,
                                 free.get((key, "ring", r)))
                    free[("stage", i)] = ma
                    slots[(n, j, key)] = ma
            return f

        parts = [[] for _ in range(12)]
        if half == 0:
            parts[0].append(xproj)
        parts[1].append(dt)
        parts[3].append(dlm)
        parts[4].append(dlum)
        parts[7].append(bc(0))
        parts[9].append(bc(1))
        parts[10].append(bc(2))
        if half == 0:
            parts[3].append(reps(0))
            parts[6].append(reps(1))
            parts[8].append(reps(2))
            parts[11].append(reps(3))
        return parts

    st_sx = [None]
    st_dts = [None]

    def unit(n, g, j, un):
        b, k, ci, half = steps[n]
        r = slots[(n, j)]
        ae = ((k * 2 + half) * NJ + j) * NG + g
        cc = (half * NJ + j) * NG + g
        e_, h_, c_ = un % NE, un % NH, un % NC_
        m_e = P.ac.op(lambda e: e.activation(E[:, e_, :], dlr[:, r, :], ACT.Exp, scale=am[:, ae:ae + 1]),
                      slots[(n, j, "dl")], free.get(("E", e_)), m_am)
        if g == NG - 1:
            free[("dl", "ring", r)] = m_e
        m = P.ve.op(lambda e: e.tensor_tensor(dbu, dur[:, r, :], rep[:, g, 0, :], ALU.mult),
                    slots[(n, j, "dlu")], rep_ready[(g, 0)], free.get("dbu"))
        if g == NG - 1:
            free[("dlu", "ring", r)] = m
        rep_used[(g, 0)] = m
        init = 0.0 if ci == 0 else car[:, cc:cc + 1]
        if k < 2:
            def scan(e):
                return e.tensor_tensor_scan(H[:, h_, :], E[:, e_, :], dbu, init, ALU.mult, ALU.add)
            last = TC - 1
        else:
            def scan(e):
                return e.tensor_tensor_scan(H[:, h_, ::-1], E[:, e_, ::-1], dbu[:, ::-1], init, ALU.mult, ALU.add)
            last = 0
        m_h = P.ve.op(scan, m, m_e, free.get(("H", h_)), free.get(("Hcar", h_)), free.get(("car", cc)))
        free["dbu"] = m_h
        free[("E", e_)] = m_h
        free[("HH", h_)] = m_h
        m_p = P.po.op(lambda e: e.tensor_tensor(HC[:, c_, :], H[:, h_, :], rep[:, g, 1, :], ALU.mult),
                      m_h, rep_ready[(g, 1)], free.get(("HC", c_)))
        rep_used[(g, 1)] = m_p
        free[("H", h_)] = m_p
        if ci < NCH - 1:
            carries.append((h_, cc, last, m_h))
        group.append((c_, j, m_p))
        if j == NJ - 1:
            items = list(group)
            group.clear()

            def mm(e, items=items):
                for sub in range(2):
                    for (c, jj, _) in items:
                        x = e.matmul(yps[32 * jj:32 * jj + 32, sub * 512:(sub + 1) * 512], sely[:],
                                     HC[:, c, sub * 512:(sub + 1) * 512], start=(g == 0), stop=(g == NG - 1))
                return x
            m = P.pe.op(mm, m_p, free.get("yps") if g == 0 else None)
            for (c, _, _) in items:
                free[("HC", c)] = m
            free["ydone"] = m

    group = []
    carries = []

    def carry():
        while carries:
            h_, cc, last, m_h = carries.pop(0)
            m = P.ac.op(lambda e, h_=h_, cc=cc, last=last: e.copy(car[:, cc:cc + 1], H[:, h_, last:last + 1]), m_h)
            free[("car", cc)] = m
            free[("Hcar", h_)] = m

    def yadd(n, done):
        b, k, ci, half = steps[n]
        t0 = t_of(k, ci)
        m = P.ve.op(lambda e: e.tensor_tensor(view(ya, k, half, t0), view(ya, k, half, t0), shaped(yps[0:C, :], k), ALU.add),
                    done, *m_yinit[b])
        free["yps"] = m
        return m

    load_u(0)
    for part in prep(0):
        for f in part:
            f()
    un = 0
    m_out = []
    pend = None
    for n, (b, k, ci, half) in enumerate(steps):
        nxt = prep(n + 1) if n + 1 < len(steps) and steps[n + 1][0] == b else None
        first = (k, ci, half) == (0, 0, 0)
        for x in range(12):
            g, j = divmod(x, NJ)
            unit(n, g, j, un)
            un += 1
            if x == 1 and pend is not None:
                pend()
                pend = None
            if first and x == 2:
                m_yinit[b] = [P.ac.op(lambda e, h=h: e.activation(ya[:, h, :], u[:, h, :], ACT.Copy, scale=dsum[:, h:h + 1]),
                                      *m_u[b], *m_out, m_ds) for h in range(2)]
                u_reads.extend(m_yinit[b])
            if nxt:
                for f in nxt[x]:
                    f()
            if len(carries) > 1 or (carries and x == 11):
                keep = [] if x == 11 else [carries.pop()]
                carry()
                carries.extend(keep)
        last_of_b = (k, ci, half) == (NK - 1, NCH - 1, 1)
        if last_of_b:
            m = yadd(n, free["ydone"])
            m_out = [P.st.dma(S["ya"][b, h], ya[:, h, :], m) for h in range(2)]
            if b + 1 < NB:
                load_u(b + 1)
                u_reads.clear()
                for part in prep(n + 1):
                    for f in part:
                        f()
        else:
            pend = lambda n=n, done=free["ydone"]: yadd(n, done)
    P.run()


def post_phase(nc, P, T, S):
    jm = T("jm", [C, C])
    lng = T("lng", [C, 2])
    lnb = T("lnb", [C, 2])
    eps = T("eps2", [C, 1])
    wo = T("wo", [C, 2, C])
    w1t = T("w1t", [C, HID])
    w1n = T("w1n", [128, 3, C])
    b1 = T("b1", [128, 3])
    w2t = T("w2t", [128, 3, C])
    w2s = T("w2s", [128, 3, C])
    w2c = T("w2c", [128, 3, C])
    co = T("co", [128, 3, 3])
    b2 = T("b2", [1, C])
    ut = T("ut", [64, 128])
    dn = T("dn", [128, 64])
    g2 = T("g2", [C, C])
    one = T("one", [64, 64])
    mt = T("mt", [C, C])
    m_c = [P.ld.dma(a[:], S[n]) for a, n in ((jm, "jmat"), (lng, "lng"), (lnb, "lnb"), (wo, "woT"), (w1t, "w1T"),
                                             (w1n, "w1n"), (b1, "b1"), (w2t, "w2T"), (co, "coef"), (b2, "b2"),
                                             (ut, "upT"), (dn, "dnT"), (g2, "gmat2"))]
    m_k = [P.ve.op(lambda e: e.memset(eps[:], 1e-5)), P.ve.op(lambda e: e.memset(one[:], 1.0))]
    for m3 in range(3):
        m_k.append(P.ve.op(lambda e, m3=m3: e.tensor_scalar(w2s[:, m3, :], w2t[:, m3, :], co[:, m3, 2:3], None, ALU.mult), *m_c))
        m_k.append(P.ve.op(lambda e, m3=m3: e.tensor_scalar(w2c[:, m3, :], w2t[:, m3, :], co[:, m3, 1:2], None, ALU.mult)))
    ps = S["psum"]
    ps_free = [None] * 8
    pi = [0]

    def bank():
        g = pi[0] % 8
        pi[0] += 1
        return g, ps_free[g]

    g, fr = bank()

    def mm(e, g=g):
        for m3 in range(3):
            x = e.matmul(ps[g][0:C, 0:C], w1n[:, m3, :], w2c[:, m3, :], start=(m3 == 0), stop=(m3 == 2))
        return x
    m = P.pe.op(mm, *m_k, *m_c)
    m_mt = ps_free[g] = P.ve.op(lambda e, g=g: e.tensor_copy(mt[:], ps[g][0:C, 0:C]), m)

    y = T("y", [C, 2, L])
    sz = T("szt", [C, 2, 2, 512])
    x1 = T("x1", [64, HW, C])
    t1 = T("t1", [128, C * 128])
    t2 = T("t2", [128, 128, C])
    sq = T("sq", [C, 2, 2, 512])
    rs = T("rs", [C, 2, 512])
    xu = T("xu", [C, 3, 512])
    hs = T("hs", [128, 2, 3, 512])
    s12 = T("s12", [64, 2, C])
    cm = T("cm", [C, 8])
    w1s = T("w1s", [C, HID])
    mts = T("mts", [C, C])
    b1p = T("b1p", [128, 3])
    vv = T("vv", [128, 3])
    cr = T("cr", [1, C])
    free = {}
    flip = [0]

    def evac(fn_a, fn_v, *marks):
        flip[0] += 1
        if flip[0] % 2:
            return P.ac.op(fn_a, *marks)
        return P.ve.op(fn_v, *marks)

    def copy2(dst, src, *marks):
        return evac(lambda e: e.copy(dst, src), lambda e: e.tensor_copy(dst, src), *marks)

    for b in range(NB):
        m_y = [P.ld.dma(y[:, h, :], S["ya"][b, h], free.get("y")) for h in range(2)]
        m_x1 = P.ld.dma(x1[:].rearrange("p w c -> p (w c)"), S["xh"][b], free.get("x1"))
        m_yd = None
        for q in range(8):
            s = q % 2
            sl = slice(q * 512, (q + 1) * 512)
            m_z = [P.ld.dma(sz[:, s, h, :], S["sz"][b, h, :, sl], free.get(("sz", s))) for h in range(2)]
            g, fr = bank()

            def mm(e, g=g, sl=sl):
                for h in range(2):
                    x = e.matmul(ps[g][0:C, :], jm[:], y[:, h, sl], start=(h == 0), stop=(h == 1))
                return x
            m = P.pe.op(mm, fr, *m_y, *m_c)
            for h in range(2):
                m = P.ve.op(lambda e, g=g, h=h, sl=sl: e.tensor_tensor(y[:, h, sl], y[:, h, sl], ps[g][0:C, :], ALU.subtract), m)
            ps_free[g] = m
            m = P.ac.op(lambda e, s=s, sl=sl: e.activation(sq[:, s, :, :], y[:, :, sl], ACT.Square), m, free.get(("sq", s)))
            g, fr = bank()

            def mm2(e, g=g, s=s):
                for h in range(2):
                    x = e.matmul(ps[g][0:C, :], jm[:], sq[:, s, h, :], start=(h == 0), stop=(h == 1))
                return x
            m = free[("sq", s)] = P.pe.op(mm2, fr, m)
            m = P.ac.op(lambda e, g=g, s=s: e.activation(rs[:, s, :], ps[g][0:C, :], ACT.Ln, bias=eps[:]), m, *m_k,
                        free.get(("rs", s)))
            ps_free[g] = m
            m = P.ac.op(lambda e, s=s: e.activation(rs[:, s, :], rs[:, s, :], ACT.Exp, scale=-0.5), m)
            for h in range(2):
                mh = P.ve.op(lambda e, h=h, s=s, sl=sl: e.tensor_tensor(y[:, h, sl], y[:, h, sl], rs[:, s, :], ALU.mult), m)
            free[("rs", s)] = mh
            for h in range(2):
                m = P.ac.op(lambda e, h=h, sl=sl: e.activation(y[:, h, sl], y[:, h, sl], ACT.Identity,
                                                               bias=lnb[:, h:h + 1], scale=lng[:, h:h + 1]), mh)
            for h in range(2):
                m_yd = P.po.op(lambda e, h=h, s=s, sl=sl: e.tensor_tensor(y[:, h, sl], y[:, h, sl], sz[:, s, h, :], ALU.mult),
                               m, *m_z)
            free[("sz", s)] = m_yd
        yv = y[:].rearrange("p a (h w) -> p a w h", w=HW)
        for w0 in range(0, HW, 4):
            g, fr = bank()

            def mm(e, g=g, w0=w0):
                for w in range(4):
                    for h in range(2):
                        x = e.matmul(ps[g][0:64, w * C:(w + 1) * C], yv[:, h, w0 + w, :], wo[:, h, :],
                                     start=(h == 0), stop=(h == 1))
                return x
            m = P.pe.op(mm, fr, m_yd)
            free["y"] = m
            m = ps_free[g] = P.ve.op(lambda e, g=g, w0=w0: e.tensor_tensor(
                x1[:, w0:w0 + 4, :], x1[:, w0:w0 + 4, :],
                ps[g][0:64, 0:4 * C].rearrange("p (w c) -> p w c", c=C), ALU.add), m, m_x1)
        m_x = m
        xsq = t1[0:64, 0:HW * C].rearrange("p (w c) -> p w c", c=C)
        ma = P.ac.op(lambda e: e.activation(xsq, x1[:], ACT.Square), m_x, free.get("t1"))
        m1 = P.ve.op(lambda e: e.tensor_reduce(s12[:, 0, :], x1[:].rearrange("p w c -> p c w"), AX.X, ALU.add), m_x,
                     free.get("s12"))
        m2 = P.ve.op(lambda e: e.tensor_reduce(s12[:, 1, :], xsq.rearrange("p w c -> p c w"), AX.X, ALU.add), ma)
        m_t1 = m2
        g, fr = bank()

        def mm(e, g=g):
            for i in range(2):
                x = e.matmul(ps[g][0:C, i:i + 1], s12[:, i, :], one[:, 0:1], start=True, stop=True)
            return x
        m = free["s12"] = P.pe.op(mm, fr, m1, m2)
        m = ps_free[g] = P.ve.op(lambda e, g=g: e.tensor_copy(cm[:, 0:2], ps[g][0:C, 0:2]), m, free.get("cm"))
        g, fr = bank()
        m = P.pe.op(lambda e, g=g: e.matmul(ps[g][0:C, 0:2], g2[:], cm[:, 0:2], start=True, stop=True), fr, m)
        m = ps_free[g] = P.ve.op(lambda e, g=g: e.tensor_copy(cm[:, 2:4], ps[g][0:C, 0:2]), m)
        m = P.ve.op(lambda e: e.scalar_tensor_tensor(cm[:, 4:5], cm[:, 2:3], cm[:, 2:3], cm[:, 3:4], ALU.mult, ALU.subtract), m)
        m = P.ac.op(lambda e: e.activation(cm[:, 5:6], cm[:, 4:5], ACT.Ln, bias=eps[:], scale=-1.0), m)
        m = P.ac.op(lambda e: e.activation(cm[:, 6:7], cm[:, 5:6], ACT.Exp, scale=-0.5), m)
        m = P.ve.op(lambda e: e.scalar_tensor_tensor(cm[:, 7:8], cm[:, 2:3], -1.0, cm[:, 6:7], ALU.mult, ALU.mult), m)
        m_w1 = P.ve.op(lambda e: e.tensor_scalar(w1s[:], w1t[:], cm[:, 6:7], None, ALU.mult), m, free.get("w1s"))
        m_ms = P.ve.op(lambda e: e.tensor_scalar(mts[:], mt[:], cm[:, 6:7], None, ALU.mult), m, m_mt)
        g, fr = bank()

        def mm(e, g=g):
            for i in range(3):
                x = e.matmul(ps[g][:, i:i + 1], w1t[:, i * 128:(i + 1) * 128], cm[:, 7:8], start=True, stop=True)
            return x
        m = free["cm"] = P.pe.op(mm, fr, m)
        m_b1 = ps_free[g] = P.ve.op(lambda e, g=g: e.tensor_tensor(b1p[:], ps[g][:, 0:3], b1[:], ALU.add), m, free.get("b1p"))
        m = P.ve.op(lambda e: e.tensor_tensor(vv[:], b1p[:], co[:, :, 1], ALU.mult), m_b1, free.get("vv"))
        m = P.ve.op(lambda e: e.tensor_tensor(vv[:], vv[:], co[:, :, 0], ALU.add), m)
        g, fr = bank()

        def mm(e, g=g):
            for i in range(3):
                x = e.matmul(ps[g][0:1, 0:C], vv[:, i:i + 1], w2t[:, i, :], start=(i == 0), stop=(i == 2))
            return x
        m = free["vv"] = P.pe.op(mm, fr, m)
        m_cr = ps_free[g] = P.ve.op(lambda e, g=g: e.tensor_tensor(cr[:], ps[g][0:1, 0:C], b2[:], ALU.add), m, free.get("cr"))

        for c0 in range(0, C, 4):
            g, fr = bank()

            def mm(e, g=g, c0=c0):
                for i in range(4):
                    x = e.matmul(ps[g][0:64, i * 128:(i + 1) * 128], x1[:, :, c0 + i], ut[:], start=True, stop=True)
                return x
            m = P.pe.op(mm, fr, m_x)
            m = ps_free[g] = copy2(t1[0:64, c0 * 128:(c0 + 4) * 128], ps[g][0:64, :], m, m_t1)
            if c0 % 8 == 0:
                m_a = m
        m_t = (m_a, m)
        t1v = t1[0:64, :].rearrange("p (c h) -> p c h", h=128)
        for h0 in range(0, 128, 4):
            q = h0 // 4
            g, fr = bank()

            def mm(e, g=g, h0=h0):
                for i in range(4):
                    x = e.matmul(ps[g][0:C, i * 128:(i + 1) * 128], t1v[:, :, h0 + i], ut[:], start=True, stop=True)
                return x
            m = P.pe.op(mm, fr, *m_t)
            free["t1"] = m
            m_xu = ps_free[g] = P.ve.op(lambda e, g=g, q=q: e.tensor_copy(xu[:, q % 3, :], ps[g][0:C, :]), m,
                                        free.get(("xu", q % 3)))
            hh = q % 2
            for m3 in range(3):
                g, fr = bank()
                m = P.pe.op(lambda e, g=g, m3=m3, q=q: e.matmul(ps[g][:, :], w1s[:, m3 * 128:(m3 + 1) * 128],
                                                                xu[:, q % 3, :], start=True, stop=True), fr, m_xu, m_w1)
                free["w1s"] = m
                m = ps_free[g] = P.ac.op(lambda e, g=g, m3=m3, hh=hh: e.activation(
                    hs[:, hh, m3, :], ps[g][:, :], ACT.Square, bias=b1p[:, m3:m3 + 1]), m, m_b1, free.get(("hs", hh)))
                free["b1p"] = m
            g, fr = bank()

            def mm(e, g=g, q=q, hh=hh):
                for i in range(4):
                    for m3 in range(3):
                        e.matmul(ps[g][:, i * C:(i + 1) * C], hs[:, hh, m3, i * 128:(i + 1) * 128], w2s[:, m3, :],
                                 start=(m3 == 0), stop=False)
                    x = e.matmul(ps[g][:, i * C:(i + 1) * C], xu[:, q % 3, i * 128:(i + 1) * 128], mts[:],
                                 start=False, stop=True)
                return x
            m = P.pe.op(mm, fr, m, m_ms)
            free[("xu", q % 3)] = free[("hs", hh)] = m
            m_t2 = ps_free[g] = P.ve.op(lambda e, g=g, h0=h0: e.tensor_copy(
                t2[:, h0:h0 + 4, :].rearrange("p h c -> p (h c)"), ps[g][:, 0:4 * C]), m, free.get("t2"))
        t3 = t1[:, 0:C * HW]
        for c0 in range(0, C, 8):
            g, fr = bank()

            def mm(e, g=g, c0=c0):
                for i in range(8):
                    x = e.matmul(ps[g][:, i * 64:(i + 1) * 64], t2[:, :, c0 + i], dn[:], start=True, stop=True)
                return x
            m = P.pe.op(mm, fr, m_t2)
            free["t2"] = m
            m = ps_free[g] = P.ac.op(lambda e, g=g, c0=c0: e.copy(t3[:, c0 * 64:(c0 + 8) * 64], ps[g][:, :]), m,
                                     free["t1"])
            g, fr = bank()

            def mm(e, g=g, c0=c0):
                e.matmul(ps[g][0:64, :], dn[:], t3[:, c0 * 64:(c0 + 8) * 64], start=True, stop=False)
                return e.matmul(ps[g][0:64, :], one[0:1, :], cr[0:1, c0:c0 + 8].unsqueeze(2).to_broadcast([1, 8, 64]),
                                start=False, stop=True)
            m = P.pe.op(mm, fr, m, m_cr)
            m = ps_free[g] = P.ve.op(lambda e, g=g, c0=c0: e.tensor_tensor(
                x1[:, :, c0:c0 + 8].rearrange("p w c -> p c w"), x1[:, :, c0:c0 + 8].rearrange("p w c -> p c w"),
                ps[g][0:64, :].rearrange("p (c w) -> p c w", w=64), ALU.add), m)
        free["t1"] = free["cr"] = (P.pe.sem, P.pe.n)
        free["x1"] = P.st.dma(S["out"][b], x1[:].rearrange("p w c -> p (w c)"), m)
    P.run()


CONSTS = ["gmat", "gmat2", "jmat", "selb", "seld", "sely", "upT", "dnT"]


def build_program(nc, S):
    with ExitStack() as top:
        psum = top.enter_context(nc.psum_tensor("psum", [128, 4096], F32))
        S["psumall"] = psum
        S["psum"] = [psum[:, i * 512:(i + 1) * 512] for i in range(8)]
        for name, shape in (("xa", [NB, 2, C, L]), ("sz", [NB, 2, C, L]), ("ya", [NB, 2, C, L])):
            S[name] = nc.dram_tensor(f"scr_{name}", shape, F32, kind="Internal").ap()
        for name, phase in (("pre", pre_phase), ("scan", scan_phase), ("post", post_phase)):
            with ExitStack() as ctx:
                def T(n, shape, dt=F32):
                    return ctx.enter_context(nc.sbuf_tensor(n, shape, dt))
                phase(nc, Phase(nc, ctx, name), T, S)


def constants():
    f = np.float32
    group = np.kron(np.eye(32), np.ones((3, 3)))
    ni, d = np.meshgrid(np.arange(4), np.arange(32), indexing="ij")
    p = (ni * 32 + d).ravel()
    selb = np.zeros((C, 8, 128), f)
    for g in range(4):
        for c in range(2):
            src = c * 16 + g * 4 + ni.ravel()
            selb[src, 2 * g + c, p] = 1
            selb[64 + src, 2 * g + c, p] = 1
    seld = np.zeros((C, 3, 128), f)
    for j in range(3):
        seld[32 * j + d.ravel(), j, p] = 1
    sely = np.zeros((128, 32), f)
    sely[p, d.ravel()] = 1

    def mask(edge):
        r = np.ones(128)
        r[33:96] = 0
        r[32] = r[96] = edge
        return r

    def operator(edge):
        return np.real(np.fft.ifft(np.fft.fft(np.eye(128), axis=0) * mask(edge)[:, None], axis=0))
    up = 2 * operator(1.0)[:, ::2]
    dn = operator(0.5)[::2, :]
    return {"gmat": (group / 3).astype(f), "gmat2": (group / (3 * L)).astype(f),
            "jmat": np.full((C, C), 1 / ND, f), "selb": selb, "seld": seld, "sely": sely,
            "upT": np.ascontiguousarray(up.T).astype(f), "dnT": np.ascontiguousarray(dn.T).astype(f)}


def lay_out(i):
    k = {n: np.asarray(v) for n, v in i.items()}
    x = k["x"]
    wi = k["L0_conv_in_proj_w"]
    xp = k["L0_conv_x_proj_w"]
    wx = np.zeros((NK, C, ND), np.float32)
    wx[:, 0:32] = xp[:, 6:38]
    wx[:, 32:38] = xp[:, 0:6]
    wx[:, 64:96] = xp[:, 6:38]
    a = {
        "xT": x.reshape(NB, L, C).transpose(0, 2, 1),
        "xh": x.reshape(NB, HW, HW * C),
        "winT": wi.T,
        "cwr": np.broadcast_to(k["L0_conv_conv_w"].reshape(ND, 9).T[None], (C, 9, ND)),
        "cb": k["L0_conv_conv_b"].reshape(2, C).T,
        "wx": wx.reshape(NK, C, 2, C).transpose(3, 0, 2, 1),
        "dtw": k["L0_conv_dt_proj_w"].transpose(2, 0, 1).reshape(NR, NK * ND),
        "dtb": k["L0_conv_dt_proj_b"].reshape(NK, 2, C).transpose(2, 0, 1).reshape(C, NK * 2),
        "ds": k["L0_conv_Ds"].reshape(NK, 2, C).transpose(2, 1, 0),
        "alog": k["L0_conv_A_logs"].reshape(NK, 2, NJ, 32, NG, 4).transpose(5, 3, 0, 1, 2, 4).reshape(128, -1),
        "lng": k["L0_conv_ln_g"].reshape(2, C).T,
        "lnb": k["L0_conv_ln_b"].reshape(2, C).T,
        "woT": k["L0_conv_out_proj_w"].T.reshape(2, C, C).transpose(1, 0, 2),
        "w1T": k["L1_conv_W1"].T,
        "w1n": k["L1_conv_W1"].reshape(3, 128, C).transpose(1, 0, 2),
        "b1": k["L1_conv_b1"].reshape(3, 128).T,
        "w2T": k["L1_conv_W2"].T.reshape(3, 128, C).transpose(1, 0, 2),
        "coef": k["L1_conv_coef"].reshape(3, 128, 3).transpose(1, 0, 2),
        "b2": k["L1_conv_b2"].reshape(1, C),
    }
    return {n: np.ascontiguousarray(v) for n, v in a.items()}


def kernel(**inputs):
    import concourse.bacc as _bacc
    from concourse.bass_utils import run_bass_kernel_spmd as _run

    data = lay_out(inputs)
    data.update(constants())
    nc = _bacc.Bacc("TRN2", target_bir_lowering=False, num_devices=1)
    arrays, S = {}, {}
    for name, a in data.items():
        arrays[f"in_{name}"] = a
        S[name] = nc.dram_tensor(f"in_{name}", a.shape, mybir.dt.from_np(a.dtype), kind="ExternalInput").ap()
    S["out"] = nc.dram_tensor("out_0_dram", (NB, HW, HW * C), F32, kind="ExternalOutput").ap()
    build_program(nc, S)
    r = _run(nc, [arrays], core_ids=[0])
    return np.asarray(r.results[0]["out_0_dram"]).reshape(NB, HW, HW, C)
```

```python
from contextlib import ExitStack

import numpy as np

import concourse.bass as bass
from concourse import mybir

ALU = mybir.AluOpType
ACT = mybir.ActivationFunctionType
AX = mybir.AxisListType
F32 = mybir.dt.float32
F32R = mybir.dt.float32r

NB = 8
HW = 64
L = HW * HW
C = 96
ND = 192
NS = 16
NK = 4
NR = 6
HID = 384
PADW = HW + 2
TC = 1024
NCH = L // TC
NG = 4
NJ = 3
YLAG = 3

FILL = ["x_pe", "x_ac", "x_ve", "dt_pe", "dt_ac", "dt_ve", "dt_po", "rep0_pe", "rep0_ac", "bc0_pe", "bc0_ac",
        "bc1_pe", "bc1_ac", "bc2_pe", "bc2_ac", "rep1_pe", "rep1_ac"]
NEW_CHUNK = [(0, "x_pe"), (1, "x_ac x_ve"), (2, "dt_pe"), (3, "dt_ac"), (4, "dt_ve dt_po rep0_pe"), (6, "rep0_ac"),
             (7, "bc0_pe"), (8, "bc0_ac bc1_pe"), (9, "bc1_ac rep1_pe"), (10, "rep1_ac bc2_pe"), (11, "bc2_ac"),
             (12, "rep2_pe"), (13, "rep2_ac"), (16, "rep3_pe"), (17, "rep3_ac")]
SAME_CHUNK = [(1, "dt_pe"), (2, "dt_ac"), (3, "dt_ve dt_po"), (6, "bc0_pe"), (7, "bc0_ac"), (8, "bc1_pe"),
              (9, "bc1_ac"), (10, "bc2_pe"), (11, "bc2_ac")]
NEXT_IMAGE = [(7, "x_pe"), (8, "x_ac x_ve"), (9, "dt_pe"), (10, "dt_ac"),
              (11, "dt_ve dt_po bc0_pe bc0_ac rep0_pe rep0_ac"), (12, "bc1_pe bc1_ac"), (13, "bc2_pe bc2_ac"),
              (14, "rep1_pe rep1_ac"), (15, "rep2_pe"), (16, "rep2_ac"), (18, "rep3_pe"), (19, "rep3_ac")]
FIRST_CHUNK = [(4, "dt_pe"), (5, "dt_ac dt_ve dt_po"), (8, "bc0_pe"), (9, "bc0_ac bc1_pe"), (10, "bc1_ac bc2_pe"),
               (11, "bc2_ac")]


class Queue:

    def __init__(self, sem):
        self.sem = sem
        self.n = 0
        self.items = []
        self.waited = {}

    def wait(self, *marks):
        for m in marks:
            if m is None:
                continue
            sem, count = m
            if self.waited.get(sem.num, 0) < count:
                self.waited[sem.num] = count
                self.items.append((0, sem, count))

    def op(self, fn, *marks):
        self.wait(*marks)
        self.n += 1
        self.items.append((1, fn, self.sem, 1))
        return (self.sem, self.n)

    def emit(self, eng):
        for it in self.items:
            if it[0] == 0:
                eng.wait_ge(it[1], it[2])
            elif it[0] == 2:
                eng.preload_act_table_set("natural_log_exp_and_others")
            else:
                it[1](eng).then_inc(it[2], it[3])


class DmaRing:

    def __init__(self, queue, sems):
        self.queue = queue
        self.sems = sems
        self.counts = [0] * len(sems)
        self.i = 0

    def dma(self, out, in_, *marks):
        k = self.i % len(self.sems)
        self.i += 1
        if self.counts[k]:
            self.queue.wait((self.sems[k], self.counts[k]))
        self.queue.wait(*marks)
        self.counts[k] += 16
        self.queue.items.append((1, lambda e: e.dma_start(out, in_), self.sems[k], 16))
        return (self.sems[k], self.counts[k])

    def drain(self):
        for s, c in zip(self.sems, self.counts):
            if c:
                self.queue.wait((s, c))


class Phase:

    def __init__(self, nc, ctx, name):
        def sem(x):
            return ctx.enter_context(nc.semaphore(f"{name}_{x}"))

        self.nc = nc
        self.pe, self.ve, self.ac, self.po, self.sp = (Queue(sem(x)) for x in ("pe", "ve", "ac", "po", "sp"))
        self.ld = DmaRing(self.sp, [sem(f"ld{i}") for i in range(6)])
        self.st = DmaRing(self.sp, [sem(f"st{i}") for i in range(6)])

    def run(self):
        self.ld.drain()
        self.st.drain()
        with self.nc.Block() as block:
            @block.sync
            def _(e):
                self.sp.emit(e)

            @block.tensor
            def _(e):
                self.pe.emit(e)

            @block.vector
            def _(e):
                self.ve.emit(e)

            @block.scalar
            def _(e):
                self.ac.emit(e)

            @block.gpsimd
            def _(e):
                self.po.emit(e)


def pre_phase(nc, P, T, S):
    win, cwr, cb, gmat, eps = (T(n, s) for n, s in (
        ("win", [C, 2 * ND]), ("cwr", [C, 9, ND]), ("cb", [C, 2]), ("gmat", [C, C]), ("eps", [C, 1])))
    wtap = T("wtap", [C, 9, ND])
    m_w = [P.ld.dma(win[:], S["winT"]), P.ld.dma(cwr[:], S["cwr"]), P.ld.dma(cb[:], S["cb"]),
           P.ld.dma(gmat[:], S["gmat"])]
    m_eps = P.ve.op(lambda e: e.memset(eps[:], 1e-5))
    m_tap = None
    for t in range(9):
        m_tap = P.ve.op(lambda e, t=t: e.tensor_tensor(wtap[:, t, :], win[:, 0:ND], cwr[:, t, :], ALU.mult), *m_w)

    xt = [T(f"xt{i}", [C, L]) for i in range(2)]
    xp = [T(f"xp{i}", [C, PADW, PADW]) for i in range(2)]
    xs = [T(f"xs{i}", [C, 2048]) for i in range(4)]
    st = T("st", [C, 8, 6])
    mv = T("mv", [C, 8])
    ps = S["psum"]
    m_pad = [P.po.op(lambda e, i=i: e.memset(xp[i][:], 0.0)) for i in range(2)]
    xt_free = [None, None]
    xp_free = [None, None]
    ps_free = [None] * 8
    xs_free = [None] * 4
    mv_free = None
    pi = xi = 0
    for b in range(NB):
        s = b % 2
        m_x = P.ld.dma(xt[s][:], S["xT"][b], xt_free[s])
        for i in range(8):
            m = P.ve.op(lambda e, i=i, s=s: e.bn_stats(st[:, i, :], xt[s][:, i * 512:(i + 1) * 512]), m_x)
        m = P.ve.op(lambda e: e.bn_aggr(mv[:, 0:2], st[:].rearrange("p a b -> p (a b)")), m, mv_free)
        m = P.ve.op(lambda e: e.scalar_tensor_tensor(mv[:, 1:2], mv[:, 0:1], mv[:, 0:1], mv[:, 1:2], ALU.mult, ALU.add), m)
        g = pi % 8
        pi += 1
        m = P.pe.op(lambda e, g=g: e.matmul(ps[g][0:C, 0:2], gmat[:], mv[:, 0:2], start=True, stop=True),
                    m, m_w[3], ps_free[g])
        m = ps_free[g] = P.ve.op(lambda e, g=g: e.tensor_copy(mv[:, 2:4], ps[g][0:C, 0:2]), m)
        m = P.ve.op(lambda e: e.scalar_tensor_tensor(mv[:, 4:5], mv[:, 2:3], mv[:, 2:3], mv[:, 3:4], ALU.mult, ALU.subtract), m)
        m = P.ac.op(lambda e: e.activation(mv[:, 5:6], mv[:, 4:5], ACT.Ln, bias=eps[:], scale=-1.0), m, m_eps)
        m = P.ac.op(lambda e: e.activation(mv[:, 6:7], mv[:, 5:6], ACT.Exp, scale=-0.5), m)
        m = P.ve.op(lambda e: e.scalar_tensor_tensor(mv[:, 7:8], mv[:, 2:3], -1.0, mv[:, 6:7], ALU.mult, ALU.mult), m)
        m_n = P.ac.op(lambda e, s=s: e.activation(
            xp[s][:, 1:HW + 1, 1:HW + 1], xt[s][:].rearrange("p (h w) -> p h w", w=HW),
            ACT.Identity, bias=mv[:, 7:8], scale=mv[:, 6:7]), m, m_pad[s], xp_free[s])
        xt_free[s] = m_n
        mv_free = m_n
        for q in range(2):
            for kind in range(2):
                for half in range(2):
                    x = xi % 4
                    xi += 1
                    for r in range(4):
                        h0 = (q * 4 + r) * 8
                        g = pi % 8
                        pi += 1

                        def mm(e, g=g, s=s, h0=h0, half=half, kind=kind):
                            if kind == 1:
                                return e.matmul(ps[g][0:C, :], win[:, ND + half * C:ND + (half + 1) * C],
                                                xp[s][:, h0 + 1:h0 + 9, 1:HW + 1], start=True, stop=True)
                            for t in range(9):
                                i = e.matmul(ps[g][0:C, :], wtap[:, t, half * C:(half + 1) * C],
                                             xp[s][:, h0 + t // 3:h0 + t // 3 + 8, t % 3:t % 3 + HW],
                                             start=(t == 0), stop=(t == 8))
                            return i
                        m = P.pe.op(mm, m_n, m_tap, ps_free[g])
                        if r == 0:
                            P.ac.wait(xs_free[x])
                        bias = cb[:, half:half + 1] if kind == 0 else 0.0
                        m = ps_free[g] = P.ac.op(lambda e, g=g, x=x, r=r, bias=bias: e.activation(
                            xs[x][:, r * 512:(r + 1) * 512], ps[g][0:C, :], ACT.Silu, bias=bias), m, *m_w)
                        last_pe = (P.pe.sem, P.pe.n)
                    dst = S["xa"] if kind == 0 else S["sz"]
                    xs_free[x] = P.st.dma(dst[b, half, :, q * 2048:(q + 1) * 2048], xs[x][:], m)
        xp_free[s] = last_pe
    P.run()


def scan_phase(nc, P, T, S):
    wx = T("wx", [C, NK, 2, C])
    dtw = T("dtw", [38, NK * ND])
    dtb = T("dtb", [C, NK * 2])
    ndtb = T("ndtb", [C, NK * 2])
    c20 = T("c20", [C, 1])
    am = T("am", [128, NK * 2 * NJ * NG])
    selb = T("selb", [C, 8, 128], F32R)
    seld = T("seld", [C, NJ, 128])
    sely = T("sely", [128, 32])
    rep = T("rep", [128, NG, 2, TC])
    selbf = rep[0:C, 0, 0, :].rearrange("p (a b) -> p a b", b=128)
    m_c = [P.ld.dma(wx[:], S["wx"]), P.ld.dma(dtw[32:38, :], S["dtw"]), P.ld.dma(dtb[:], S["dtb"]),
           P.ld.dma(am[:], S["alog"]), P.ld.dma(selbf, S["selb"]),
           P.ld.dma(seld[:], S["seld"]), P.ld.dma(sely[:], S["sely"])]
    P.ac.items.append((2,))
    m = P.ac.op(lambda e: e.activation(am[:], am[:], ACT.Exp), *m_c)
    m_am = P.ac.op(lambda e: e.mul(am[:], am[:], -1.0), m)
    m_sel = P.ve.op(lambda e: e.tensor_copy(selb[:], selbf), *m_c)
    m_c20 = P.ve.op(lambda e: e.memset(c20[:], 20.0))
    m_nb = P.ve.op(lambda e: e.tensor_scalar(ndtb[:], dtb[:], -1.0, 20.0, ALU.mult, ALU.add))

    u = T("u", [C, 2, L])
    yt = T("yt", [C, 2, TC])
    NRING = 6
    dlr = T("dlr", [128, NRING, TC])
    dur = T("dur", [128, NRING, TC])
    NE, NH, NC_ = 4, 3, 6
    E = T("E", [128, NE, TC])
    H = T("H", [128, NH, TC])
    HC = T("HC", [128, NC_, TC])
    dl = T("dl", [C, TC])
    dlu = T("dlu", [C, TC])
    sx = T("sx", [C, TC], F32R)
    dts = T("dts", [38, TC])
    car = T("car", [128, 2 * NJ * NG])
    psum = S["psumall"]
    stage = [psum[:, 0:1024], psum[:, 1024:2048]]
    dbs = T("dbs", [128, TC])
    dbu = [psum[:, 2048:3072], dbs[:]]
    yps = psum[:, 3072:4096]

    free = {}
    stage_idle = [0, 1]

    def view(t, k, half, t0):
        if k % 2 == 0:
            return t[:, half, t0:t0 + TC]
        return t[:, half, :].rearrange("p (h w) -> p w h", w=HW)[:, t0 // HW:(t0 + TC) // HW, :]

    def viewn(t, k, half, t0, n):
        if k % 2 == 0:
            return t[:, half, t0:t0 + n]
        return t[:, half, :].rearrange("p (h w) -> p w h", w=HW)[:, t0 // HW:(t0 + n) // HW, :]

    def shaped(ap, k):
        return ap if k % 2 == 0 else ap.rearrange("p (w h) -> p w h", h=HW)

    def next_stage():
        i = stage_idle.pop(0)
        return i, free.get(("stage", i))

    def stage_done(i, m):
        stage_idle.append(i)
        free[("stage", i)] = m

    steps = [(b, k, ci, half) for b in range(NB) for k in range(NK) for ci in range(NCH) for half in range(2)]
    m_u = {}
    ring_n = [0]
    rep_ready = {}
    rep_used = {(0, 0): m_sel}
    slots = {}
    u_reads = []

    def t_of(k, ci):
        return TC * (ci if k < 2 else NCH - 1 - ci)

    def load_u(b):
        m_u[b] = [P.ld.dma(u[:, h, :], S["xa"][b, h], *u_reads) for h in range(2)]

    def prep(n):
        b, k, ci, half = steps[n]
        t0 = t_of(k, ci)
        st = {}
        kk = k * 2 + half

        def x_pe():
            i, fr = next_stage()

            def mm(e):
                for sub in range(2):
                    for h in range(2):
                        r = e.matmul(stage[i][0:C, sub * 512:(sub + 1) * 512], wx[:, k, h, :],
                                     viewn(u, k, h, t0 + sub * 512, 512), start=(h == 0), stop=(h == 1))
                return r
            st["x"] = i, P.pe.op(mm, fr, *m_u[b], *m_c)
            u_reads.append(st["x"][1])

        def x_ac():
            i, m = st["x"]
            st_x["dts"] = P.ac.op(lambda e: e.copy(dts[32:38, :], stage[i][32:38, :]), m, free.get("dts"))
            st["sx"] = P.ac.op(lambda e: e.copy(sx[:], stage[i][0:C, :]), m, free.get("sx"))

        def x_ve():
            i, _ = st["x"]
            m = P.ve.op(lambda e: e.tensor_tensor(sx[64:96, :], stage[i][64:96, :], sx[64:96, :], ALU.subtract),
                        st["sx"], st_x["dts"])
            st_x["sx"] = m
            stage_done(i, m)

        def rep_pe(g):
            for c in range(2):
                i, fr = next_stage()

                def mm(e, i=i, c=c):
                    for sub in range(2):
                        r = e.matmul(stage[i][:, sub * 512:(sub + 1) * 512], selb[:, 2 * g + c, :],
                                     sx[:, sub * 512:(sub + 1) * 512], start=True, stop=True)
                    return r
                m = P.pe.op(mm, fr, st_x["sx"], m_sel)
                free["sx"] = m
                st[("rep", g, c)] = i, m

        def rep_ac(g):
            for c in range(2):
                i, m = st[("rep", g, c)]
                mr = P.ac.op(lambda e, i=i, c=c: e.copy(rep[:, g, c, :], stage[i][:]), m, rep_used.get((g, c)))
                rep_ready[(g, c)] = mr
                stage_done(i, mr)

        def dt_pe():
            i, fr = next_stage()

            def mm(e):
                for sub in range(2):
                    r = e.matmul(stage[i][0:C, sub * 512:(sub + 1) * 512],
                                 dtw[32:38, k * ND + half * C:k * ND + (half + 1) * C],
                                 dts[32:38, sub * 512:(sub + 1) * 512], start=True, stop=True)
                return r
            free["dts"] = m = P.pe.op(mm, fr, st_x["dts"], *m_c)
            st["dt"] = i, m

        def dt_ac():
            i, m = st["dt"]
            m = P.ac.op(lambda e: e.activation(dlu[:], stage[i][0:C, :], ACT.Relu, bias=ndtb[:, kk:kk + 1], scale=-1.0),
                        m, free.get("dlu"), m_nb)
            m = P.ac.op(lambda e: e.activation(dlu[:], dlu[:], ACT.Exp, bias=c20[:], scale=-1.0), m, m_c20)
            st["ln"] = P.ac.op(lambda e: e.activation(dlu[:], dlu[:], ACT.Ln, bias=1.0), m)

        def dt_ve():
            i, _ = st["dt"]
            m = P.ve.op(lambda e: e.scalar_tensor_tensor(dl[:], stage[i][0:C, :], dtb[:, kk:kk + 1], dlu[:],
                                                         ALU.add, ALU.max), st["ln"], free.get("dl"))
            st["dl"] = m
            stage_done(i, m)

        def dt_po():
            st["dlu"] = P.po.op(lambda e: e.tensor_tensor(shaped(dlu[:], k), shaped(dl[:], k), view(u, k, half, t0),
                                                          ALU.mult), st["dl"], *m_u[b])
            u_reads.append(st["dlu"])

        def bc_pe(j):
            for (src, key) in ((dl, "dl"), (dlu, "dlu")):
                i, fr = next_stage()

                def mm(e, i=i, src=src):
                    for sub in range(2):
                        x = e.matmul(stage[i][:, sub * 512:(sub + 1) * 512], seld[:, j, :],
                                     src[:, sub * 512:(sub + 1) * 512], start=True, stop=True)
                    return x
                free[key] = m = P.pe.op(mm, fr, st[key])
                st[("bc", j, key)] = i, m

        def bc_ac(j):
            r = ring_n[0] % NRING
            ring_n[0] += 1
            slots[(n, j)] = r
            for (dst, key) in ((dlr, "dl"), (dur, "dlu")):
                i, m = st[("bc", j, key)]
                ma = P.ac.op(lambda e, i=i, dst=dst: e.copy(dst[:, r, :], stage[i][:]), m, free.get((key, "ring", r)))
                slots[(n, j, key)] = ma
                stage_done(i, ma)

        fs = {"x_pe": x_pe, "x_ac": x_ac, "x_ve": x_ve, "dt_pe": dt_pe, "dt_ac": dt_ac, "dt_ve": dt_ve, "dt_po": dt_po}
        for j in range(NJ):
            fs[f"bc{j}_pe"] = lambda j=j: bc_pe(j)
            fs[f"bc{j}_ac"] = lambda j=j: bc_ac(j)
        for g in range(NG):
            fs[f"rep{g}_pe"] = lambda g=g: rep_pe(g)
            fs[f"rep{g}_ac"] = lambda g=g: rep_ac(g)
        return fs

    st_x = {}

    def unit(n, g, j, un):
        b, k, ci, half = steps[n]
        r = slots[(n, j)]
        ae = ((k * 2 + half) * NJ + j) * NG + g
        e_ = un % NE
        m_e = P.ac.op(lambda e: e.activation(E[:, e_, :], dlr[:, r, :], ACT.Exp, scale=am[:, ae:ae + 1]),
                      slots[(n, j, "dl")], free.get(("E", e_)), m_am)
        if g == NG - 1:
            free[("dl", "ring", r)] = m_e
        d_ = un % 2
        m_d = P.ve.op(lambda e: e.tensor_tensor(dbu[d_], dur[:, r, :], rep[:, g, 0, :], ALU.mult),
                      slots[(n, j, "dlu")], rep_ready[(g, 0)], free.get(("dbu", d_)))
        if g == NG - 1:
            free[("dlu", "ring", r)] = m_d
        rep_used[(g, 0)] = m_d
        if pending:
            pending.pop()()
        pending.append(lambda: unit_tail(n, g, j, un, m_e, m_d))

    def unit_tail(n, g, j, un, m_e, m_d):
        b, k, ci, half = steps[n]
        cc = (half * NJ + j) * NG + g
        e_, h_, c_, d_ = un % NE, un % NH, un % NC_, un % 2
        init = 0.0 if ci == 0 else car[:, cc:cc + 1]
        if k < 2:
            def scan(e):
                return e.tensor_tensor_scan(H[:, h_, :], E[:, e_, :], dbu[d_], init, ALU.mult, ALU.add)
            last = TC - 1
        else:
            def scan(e):
                return e.tensor_tensor_scan(H[:, h_, ::-1], E[:, e_, ::-1], dbu[d_][:, ::-1], init, ALU.mult, ALU.add)
            last = 0
        m_h = P.ve.op(scan, m_d, m_e, free.get(("H", h_)), free.get(("Hcar", h_)), free.get(("car", cc)))
        free[("dbu", d_)] = m_h
        free[("E", e_)] = m_h
        m_p = P.po.op(lambda e: e.tensor_tensor(HC[:, c_, :], H[:, h_, :], rep[:, g, 1, :], ALU.mult),
                      m_h, rep_ready[(g, 1)], free.get(("HC", c_)))
        rep_used[(g, 1)] = m_p
        free[("H", h_)] = m_p

        def carry():
            free[("car", cc)] = free[("Hcar", h_)] = P.ac.op(
                lambda e: e.copy(car[:, cc:cc + 1], H[:, h_, last:last + 1]), m_h)
        if ci < NCH - 1:
            at(un + 2, carry)
        group.append((c_, j, m_p))
        if j == NJ - 1:
            items = list(group)
            group.clear()

            def mm(e):
                for sub in range(2):
                    for (c, jj, _) in items:
                        x = e.matmul(yps[32 * jj:32 * jj + 32, sub * 512:(sub + 1) * 512], sely[:],
                                     HC[:, c, sub * 512:(sub + 1) * 512], start=(g == 0), stop=(g == NG - 1))
                return x

            def ysum():
                m = P.pe.op(mm, m_p, free.get("yps") if g == 0 else None)
                for (c, _, _) in items:
                    free[("HC", c)] = m
                free["ydone"] = m
            at(un + YLAG, ysum)

    group = []
    pending = []
    events = {}

    def at(when, fn):
        events.setdefault(when, []).append(fn)

    def yout(n):
        b, k, ci, half = steps[n]
        t0 = t_of(k, ci)
        i = n % 2
        m = P.ac.op(lambda e: e.copy(yt[:, i, :], yps[0:C, :]), free["ydone"], free.get(("yt", i)))
        free["yps"] = m
        free[("yt", i)] = P.st.dma(S["yk"][b, k, half, :, t0:t0 + TC], yt[:, i, :], m)

    load_u(0)
    fs = prep(0)
    for name in FILL:
        fs[name]()
    for g in (2, 3):
        at(6 * g - 12, fs[f"rep{g}_pe"])
        at(6 * g - 11, fs[f"rep{g}_ac"])
    un = 0
    for n, (b, k, ci, half) in enumerate(steps):
        at(un + 12 + YLAG, lambda n=n: yout(n))
        if n + 1 < len(steps):
            nb, _, _, nh = steps[n + 1]
            fs = prep(n + 1)
            if nb != b:
                u_done = list(u_reads)
                u_reads.clear()
                m_u[nb] = [P.ld.dma(u[:, h, :], S["xa"][nb, h], *u_done) for h in range(2)]
            plan = NEXT_IMAGE if nb != b else NEW_CHUNK if nh == 0 else FIRST_CHUNK if (k, ci) == (0, 0) else SAME_CHUNK
            for x, names in plan:
                for name in names.split():
                    at(un + x, fs[name])
        for x in range(12):
            unit(n, x // NJ, x % NJ, un)
            for f in events.pop(un, ()):
                f()
            un += 1
    pending.pop()()
    while events:
        for f in events.pop(min(events)):
            f()
    P.run()


def skewed(count, *stages):
    for t in range(count + len(stages) - 1):
        for s in reversed(range(len(stages))):
            if 0 <= t - s < count:
                stages[s](t - s)
        yield


def post_phase(nc, P, T, S):
    jm = T("jm", [C, C])
    lng = T("lng", [C, 2])
    lnb = T("lnb", [C, 2])
    eps = T("eps2", [C, 1])
    wo = T("wo", [C, 2, 128])
    w1t = T("w1t", [C, HID])
    b1 = T("b1", [128, 3])
    w2t = T("w2t", [128, 3, C])
    w2s = T("w2s", [128, 3, 128])
    co = T("co", [128, 3, 3])
    b2 = T("b2", [1, C])
    ut = T("ut", [128, 128])
    dn = T("dn", [128, 128])
    g2 = T("g2", [C, C])
    one = T("one", [128, 64])
    mt = T("mt", [C, C])
    ds = T("ds", [C, 2, NK])
    dsum = T("dsum", [C, 2])
    y = T("y", [128, 2, L])
    x1 = T("x1", [128, HW, C])
    t1 = T("t1", [128, C * 128])
    t2 = T("t2", [128, 128, C])
    tmp = T("tmp", [C, 2, 1024])
    sz = T("szt", [C, 2, 2, 512])
    sq = T("sq", [C, 2, 512])
    rs = T("rs", [C, 2, 512])
    xu = T("xu", [C, 2, 512])
    hs = T("hs", [128, 2, 3, 512])
    s12 = T("s12", [128, 2, C])
    cm = T("cm", [C, 8])
    w1s = T("w1s", [C, 2, HID])
    mts = T("mts", [C, 2, 128])
    b1p = T("b1p", [128, 2, 3])
    vv = T("vv", [128, 3])
    cr = T("cr", [1, 2, C])
    w1n, w2c = t2[:, 0:3, :], t2[:, 3:6, :]
    m_c = [P.ld.dma(a, S[n]) for a, n in ((jm[:], "jmat"), (lng[:], "lng"), (lnb[:], "lnb"), (wo[:], "woT"),
                                          (w1t[:], "w1T"), (w1n, "w1n"), (b1[:], "b1"), (w2t[:], "w2T"),
                                          (co[:], "coef"), (b2[:], "b2"), (ut[0:64, :], "upT"), (ut[64:128, :], "upT"),
                                          (dn[:], "dnT"), (g2[:], "gmat2"), (ds[:], "ds"))]
    m_eps = P.ve.op(lambda e: e.memset(eps[:], 1e-5))
    m_one = P.ve.op(lambda e: e.memset(one[:], 1.0))
    m_ds = P.ve.op(lambda e: e.tensor_reduce(dsum[:], ds[:], AX.X, ALU.add), *m_c)
    m_w2z = P.ve.op(lambda e: e.memset(w2s[:], 0.0))
    m_mtz = P.ve.op(lambda e: e.memset(mts[:], 0.0))
    for i in range(3):
        m_w2s = P.ve.op(lambda e, i=i: e.tensor_scalar(w2s[:, i, 0:C], w2t[:, i, :], co[:, i, 2:3], None, ALU.mult), m_w2z)
        m = P.ve.op(lambda e, i=i: e.tensor_scalar(w2c[:, i, :], w2t[:, i, :], co[:, i, 1:2], None, ALU.mult))
    ps = S["psum"]
    ps_free = [None] * 8
    turn = [0]
    free = {}
    done = {}

    def bank():
        g = turn[0] % 8
        turn[0] += 1
        return g, ps_free[g]

    def matmuls(g, fr, calls, *marks):
        def mm(e):
            for (o, l, r, first, last) in calls:
                x = e.matmul(o, l, r, start=first, stop=last)
            return x
        return P.pe.op(mm, fr, *marks)

    g, fr = bank()
    m = matmuls(g, fr, [(ps[g][0:C, 0:C], w1n[:, i, :], w2c[:, i, :], i == 0, i == 2) for i in range(3)], m, *m_c)
    free["t2"] = m
    m_mt = ps_free[g] = P.ve.op(lambda e: e.tensor_copy(mt[:], ps[0][0:C, 0:C]), m)

    def gather(b):
        p = b % 2
        lo, hi = 64 * p, 64 * p + 64
        xb = x1[lo:hi, :, :]
        m_x1 = P.ld.dma(xb.rearrange("p w c -> p (w c)"), S["xh"][b], free.get(("x1", p)))
        m_y = []
        st = {}
        m_0 = [P.ld.dma(y[0:C, h, :], S["yk"][b, 0, h], free.get("y")) for h in range(2)]
        terms = [(h, k, part) for h in range(2) for k in (2, 0, 1, 3) for part in range(4)]

        def load(n):
            h, k, part = terms[n]
            src = S["yk"][b, k, h] if k else S["xa"][b, h]
            st[n] = P.ld.dma(tmp[:, n % 2, :], src[:, part * 1024:(part + 1) * 1024], free.get(("tmp", n % 2)))

        def add(n):
            h, k, part = terms[n]
            w = tmp[:, n % 2, :]
            if k % 2:
                v = y[0:C, h, :].rearrange("p (h w) -> p w h", w=HW)[:, part * 16:part * 16 + 16, :]
                w = w.rearrange("p (w h) -> p w h", h=HW)
            else:
                v = y[0:C, h, part * 1024:(part + 1) * 1024]
            before = st.get("add", m_0[0])
            if k:
                m = P.ve.op(lambda e: e.tensor_tensor(v, v, w, ALU.add), st[n], before, *m_0)
            else:
                m = P.ve.op(lambda e: e.scalar_tensor_tensor(v, w, dsum[:, h:h + 1], v, ALU.mult, ALU.add),
                            st[n], before, m_ds, *m_0)
            free[("tmp", n % 2)] = st["add"] = m

        yield from skewed(len(terms), load, add)
        m_sum = st["add"]

        def mean(q):
            sl = slice(q * 512, (q + 1) * 512)
            st[("z", q)] = [P.ld.dma(sz[:, q % 2, h, :], S["sz"][b, h, :, sl], free.get(("sz", q % 2))) for h in range(2)]
            g, fr = bank()
            m = matmuls(g, fr, [(ps[g][0:C, :], jm[:], y[0:C, h, sl], h == 0, h == 1) for h in range(2)], m_sum, *m_c)
            for h in range(2):
                m = P.ve.op(lambda e, h=h: e.tensor_tensor(y[0:C, h, sl], y[0:C, h, sl], ps[g][0:C, :], ALU.subtract), m)
            ps_free[g] = m
            st[("sq", q)] = P.ac.op(lambda e: e.activation(sq[:], y[0:C, :, sl], ACT.Square), m, free.get("sq"))
            st[("yc", q)] = m

        def var(q):
            g, fr = bank()
            free["sq"] = m = matmuls(g, fr, [(ps[g][0:C, :], jm[:], sq[:, h, :], h == 0, h == 1) for h in range(2)],
                                     st[("sq", q)])
            s = q % 2
            m = ps_free[g] = P.ac.op(lambda e: e.activation(rs[:, s, :], ps[g][0:C, :], ACT.Ln, bias=eps[:]), m, m_eps,
                                     free.get(("rs", s)))
            st[("rs", q)] = P.ac.op(lambda e: e.activation(rs[:, s, :], rs[:, s, :], ACT.Exp, scale=-0.5), m)

        def scale(q):
            sl = slice(q * 512, (q + 1) * 512)
            s = q % 2
            for h in range(2):
                m = P.ve.op(lambda e, h=h: e.tensor_tensor(y[0:C, h, sl], y[0:C, h, sl], rs[:, s, :], ALU.mult), st[("rs", q)])
            free[("rs", s)] = m
            for h in range(2):
                m2 = P.ac.op(lambda e, h=h: e.activation(y[0:C, h, sl], y[0:C, h, sl], ACT.Identity,
                                                         bias=lnb[:, h:h + 1], scale=lng[:, h:h + 1]), m, *m_c)
            for h in range(2):
                m = P.po.op(lambda e, h=h: e.tensor_tensor(y[0:C, h, sl], y[0:C, h, sl], sz[:, s, h, :], ALU.mult),
                            m2, *st[("z", q)])
            free[("sz", s)] = st["y2"] = m

        yield from skewed(8, mean, var, scale)
        yv = y[0:C, :, :].rearrange("p a (h w) -> p a w h", w=HW)

        def project(n):
            w0 = 4 * n
            g, fr = bank()
            m = free["y"] = matmuls(g, fr, [(ps[g][lo:hi, w * 128:(w + 1) * 128], yv[:, h, w0 + w, :], wo[:, h, :], h == 0, h == 1)
                                            for w in range(4) for h in range(2)], st["y2"])
            st["x"] = ps_free[g] = P.ve.op(lambda e: e.tensor_tensor(
                xb[:, w0:w0 + 4, :], xb[:, w0:w0 + 4, :],
                ps[g][lo:hi, :].rearrange("p (w c) -> p w c", c=128)[:, :, 0:C], ALU.add), m, m_x1)

        yield from skewed(16, project)
        m_x = done[("x", b)] = st["x"]
        yf = y[lo:hi, :, :].rearrange("p a l -> p (a l)")[:, 0:HW * C]
        xsq = yf.rearrange("p (w c) -> p w c", c=C)
        ma = None
        for i in range(4):
            ma = P.ac.op(lambda e, i=i: e.activation(xsq[:, 16 * i:16 * i + 16, :], xb[:, 16 * i:16 * i + 16, :], ACT.Square),
                         m_x, free["y"])
            yield
        m1 = P.ve.op(lambda e: e.tensor_reduce(s12[lo:hi, 0, :], xb.rearrange("p w c -> p c w"), AX.X, ALU.add), m_x,
                     free.get("s12"))
        yield
        m2 = P.ve.op(lambda e: e.tensor_reduce(s12[lo:hi, 1, :], xsq.rearrange("p w c -> p c w"), AX.X, ALU.add), ma)
        free["y"] = m2
        yield
        g, fr = bank()
        m = free["s12"] = matmuls(g, fr, [(ps[g][0:C, i:i + 1], s12[lo:hi, i, :], one[lo:hi, 0:1], True, True) for i in range(2)],
                                  m1, m2, m_one)
        m = ps_free[g] = P.ve.op(lambda e, g=g: e.tensor_copy(cm[:, 0:2], ps[g][0:C, 0:2]), m, free.get("cm"))
        g, fr = bank()
        m = matmuls(g, fr, [(ps[g][0:C, 0:2], g2[:], cm[:, 0:2], True, True)], m)
        m = ps_free[g] = P.ve.op(lambda e, g=g: e.tensor_copy(cm[:, 2:4], ps[g][0:C, 0:2]), m)
        m = P.ve.op(lambda e: e.scalar_tensor_tensor(cm[:, 4:5], cm[:, 2:3], cm[:, 2:3], cm[:, 3:4], ALU.mult, ALU.subtract), m)
        yield
        m = P.ac.op(lambda e: e.activation(cm[:, 5:6], cm[:, 4:5], ACT.Ln, bias=eps[:], scale=-1.0), m)
        m = P.ac.op(lambda e: e.activation(cm[:, 6:7], cm[:, 5:6], ACT.Exp, scale=-0.5), m)
        yield
        m = P.ve.op(lambda e: e.scalar_tensor_tensor(cm[:, 7:8], cm[:, 2:3], -1.0, cm[:, 6:7], ALU.mult, ALU.mult), m)
        m_w = P.ve.op(lambda e: e.tensor_scalar(w1s[:, p, :], w1t[:], cm[:, 6:7], None, ALU.mult), m, free.get(("w1s", p)))
        m_m = P.ve.op(lambda e: e.tensor_scalar(mts[:, p, 0:C], mt[:], cm[:, 6:7], None, ALU.mult), m, m_mt, m_mtz, free.get(("mts", p)))
        g, fr = bank()
        m = free["cm"] = matmuls(g, fr, [(ps[g][:, i:i + 1], w1t[:, i * 128:(i + 1) * 128], cm[:, 7:8], True, True)
                                         for i in range(3)], m)
        m_b = ps_free[g] = P.ve.op(lambda e, g=g: e.tensor_tensor(b1p[:, p, :], ps[g][:, 0:3], b1[:], ALU.add), m,
                                   free.get(("b1p", p)))
        m = P.ve.op(lambda e: e.tensor_tensor(vv[:], b1p[:, p, :], co[:, :, 1], ALU.mult), m_b, free.get("vv"))
        m = P.ve.op(lambda e: e.tensor_tensor(vv[:], vv[:], co[:, :, 0], ALU.add), m)
        yield
        g, fr = bank()
        m = free["vv"] = matmuls(g, fr, [(ps[g][0:1, 0:C], vv[:, i:i + 1], w2t[:, i, :], i == 0, i == 2)
                                         for i in range(3)], m)
        m_r = ps_free[g] = P.ve.op(lambda e, g=g: e.tensor_tensor(cr[:, p, :], ps[g][0:1, 0:C], b2[:], ALU.add), m,
                                   free.get(("cr", p)))
        done[("scaled", b)] = (m_w, m_m, m_b, m_r)
        yield

    def resample(b):
        p = b % 2
        lo, hi = 64 * p, 64 * p + 64
        xb = x1[lo:hi, :, :]
        m_x = done[("x", b)]
        m_w, m_m, m_b, m_r = done[("scaled", b)]
        st = {"t1": {}}

        def up_h(n):
            c0 = 4 * n
            g, fr = bank()
            m = matmuls(g, fr, [(ps[g][0:64, i * 128:(i + 1) * 128], xb[:, :, c0 + i], ut[lo:hi, :], True, True)
                                for i in range(4)], m_x)
            to = t1[0:64, c0 * 128:(c0 + 4) * 128]
            if n % 2:
                m = P.ac.op(lambda e: e.copy(to, ps[g][0:64, :]), m, free.get("t1"))
            else:
                m = P.ve.op(lambda e: e.tensor_copy(to, ps[g][0:64, :]), m, free.get("t1"))
            ps_free[g] = st["t1"][n % 2] = m

        yield from skewed(24, up_h)
        t1v = t1[0:64, :].rearrange("p (c h) -> p c h", h=128)

        def up_w(q):
            h0 = 4 * q
            g, fr = bank()
            m = free["t1"] = matmuls(g, fr, [(ps[g][0:C, i * 128:(i + 1) * 128], t1v[:, :, h0 + i], ut[0:64, :], True, True) for i in range(4)], *st["t1"].values())
            st[("xu", q)] = ps_free[g] = P.ve.op(lambda e: e.tensor_copy(xu[:, q % 2, :], ps[g][0:C, :]), m,
                                                 free.get(("xu", q % 2)))

        def hidden(q):
            hh = q % 2
            for i in range(3):
                g, fr = bank()
                m = free[("w1s", p)] = matmuls(g, fr, [(ps[g][:], w1s[:, p, i * 128:(i + 1) * 128], xu[:, q % 2, :], True, True)],
                                               st[("xu", q)], m_w)
                m = ps_free[g] = P.ac.op(lambda e, g=g, i=i: e.activation(
                    hs[:, hh, i, :], ps[g][:], ACT.Square, bias=b1p[:, p, i:i + 1]), m, m_b, free.get(("hs", hh)))
            free[("b1p", p)] = st[("hs", q)] = m

        def back(q):
            hh = q % 2
            g, fr = bank()
            calls = []
            for i in range(4):
                o = ps[g][:, i * 128:(i + 1) * 128]
                sl = slice(i * 128, (i + 1) * 128)
                calls += [(o, xu[:, q % 2, sl], mts[:, p, :], True, False)]
                calls += [(o, hs[:, hh, j, sl], w2s[:, j, :], False, j == 2) for j in range(3)]
            m = matmuls(g, fr, calls, st[("hs", q)], m_m, m_w2s)
            free[("xu", hh)] = free[("hs", hh)] = free[("mts", p)] = m
            st["t2"] = ps_free[g] = P.ve.op(lambda e: e.tensor_copy(
                t2[:, 4 * q:4 * q + 4, :], ps[g][:].rearrange("p (h c) -> p h c", c=128)[:, :, 0:C]), m, free.get("t2"))

        for q in range(33):
            if q < 32:
                up_w(q)
            if q >= 1:
                back(q - 1)
            if q < 32:
                hidden(q)
            yield
        t3 = t1

        def down_w(n):
            g, fr = bank()
            m = free["t2"] = matmuls(g, fr, [(ps[g][:, i * 128:(i + 1) * 128], t2[:, :, 4 * n + i], dn[:], True, True)
                                             for i in range(4)], st["t2"])
            st[("t3", n)] = ps_free[g] = P.ac.op(lambda e: e.copy(
                t3[:, n * 256:(n + 1) * 256].rearrange("p (c w) -> p c w", w=64),
                ps[g][:].rearrange("p (c w) -> p c w", w=128)[:, :, 0:64]), m, free["t1"])

        def down_h(n):
            if n % 2 == 0:
                return
            c0 = 4 * n - 4
            g, fr = bank()
            m = matmuls(g, fr, [(ps[g][lo:hi, :], dn[:, 0:64], t3[:, c0 * 64:(c0 + 8) * 64], True, False),
                                (ps[g][lo:hi, :], one[0:1, :], cr[0:1, p, c0:c0 + 8].unsqueeze(2).to_broadcast([1, 8, 64]),
                                 False, True)], st[("t3", n)], st[("t3", n - 1)], m_r)
            st["pe"] = m
            xc = xb[:, :, c0:c0 + 8].rearrange("p w c -> p c w")
            st["out"] = ps_free[g] = P.ve.op(lambda e: e.tensor_tensor(
                xc, xc, ps[g][lo:hi, :].rearrange("p (c w) -> p c w", w=64), ALU.add), m)

        yield from skewed(24, down_w, down_h)
        free["t1"] = free[("cr", p)] = st["pe"]
        free[("x1", p)] = P.st.dma(S["out"][b], xb.rearrange("p w c -> p (w c)"), st["out"])

    for _ in gather(0):
        pass
    for b in range(NB):
        side = gather(b + 1) if b + 1 < NB else iter(())
        for n, _ in enumerate(resample(b)):
            for _ in range(0 if n < 24 else 2 if n < 57 else 1):
                next(side, None)
        for _ in side:
            pass
    P.run()


def build_program(nc, S):
    with ExitStack() as top:
        psum = top.enter_context(nc.psum_tensor("psum", [128, 4096], F32))
        S["psumall"] = psum
        S["psum"] = [psum[:, i * 512:(i + 1) * 512] for i in range(8)]
        for name, shape in (("xa", [NB, 2, C, L]), ("sz", [NB, 2, C, L]), ("yk", [NB, NK, 2, C, L])):
            S[name] = nc.dram_tensor(f"scr_{name}", shape, F32, kind="Internal").ap()
        for name, phase in (("pre", pre_phase), ("scan", scan_phase), ("post", post_phase)):
            with ExitStack() as ctx:
                def T(n, shape, dt=F32):
                    return ctx.enter_context(nc.sbuf_tensor(n, shape, dt))
                phase(nc, Phase(nc, ctx, name), T, S)


def constants():
    f = np.float32
    group = np.kron(np.eye(32), np.ones((3, 3)))
    ni, d = np.meshgrid(np.arange(4), np.arange(32), indexing="ij")
    p = (ni * 32 + d).ravel()
    selb = np.zeros((C, 8, 128), f)
    for g in range(4):
        for c in range(2):
            src = c * 16 + g * 4 + ni.ravel()
            selb[src, 2 * g + c, p] = 1
            selb[64 + src, 2 * g + c, p] = 1
    seld = np.zeros((C, 3, 128), f)
    for j in range(3):
        seld[32 * j + d.ravel(), j, p] = 1
    sely = np.zeros((128, 32), f)
    sely[p, d.ravel()] = 1

    def mask(edge):
        r = np.ones(128)
        r[33:96] = 0
        r[32] = r[96] = edge
        return r

    def operator(edge):
        return np.real(np.fft.ifft(np.fft.fft(np.eye(128), axis=0) * mask(edge)[:, None], axis=0))
    up = 2 * operator(1.0)[:, ::2]
    dn = operator(0.5)[::2, :]
    return {"gmat": (group / 3).astype(f), "gmat2": (group / (3 * L)).astype(f),
            "jmat": np.full((C, C), 1 / ND, f), "selb": selb, "seld": seld, "sely": sely,
            "upT": np.ascontiguousarray(up.T).astype(f),
            "dnT": np.concatenate([dn.T, np.zeros((128, 64))], axis=1).astype(f)}


def lay_out(i):
    k = {n: np.asarray(v) for n, v in i.items()}
    x = k["x"]
    wi = k["L0_conv_in_proj_w"]
    xp = k["L0_conv_x_proj_w"]
    wx = np.zeros((NK, C, ND), np.float32)
    wx[:, 0:32] = xp[:, 6:38]
    wx[:, 32:38] = xp[:, 0:6]
    wx[:, 64:96] = xp[:, 6:38]
    a = {
        "xT": x.reshape(NB, L, C).transpose(0, 2, 1),
        "xh": x.reshape(NB, HW, HW * C),
        "winT": wi.T,
        "cwr": np.broadcast_to(k["L0_conv_conv_w"].reshape(ND, 9).T[None], (C, 9, ND)),
        "cb": k["L0_conv_conv_b"].reshape(2, C).T,
        "wx": wx.reshape(NK, C, 2, C).transpose(3, 0, 2, 1),
        "dtw": k["L0_conv_dt_proj_w"].transpose(2, 0, 1).reshape(NR, NK * ND),
        "dtb": k["L0_conv_dt_proj_b"].reshape(NK, 2, C).transpose(2, 0, 1).reshape(C, NK * 2),
        "ds": k["L0_conv_Ds"].reshape(NK, 2, C).transpose(2, 1, 0),
        "alog": k["L0_conv_A_logs"].reshape(NK, 2, NJ, 32, NG, 4).transpose(5, 3, 0, 1, 2, 4).reshape(128, -1),
        "lng": k["L0_conv_ln_g"].reshape(2, C).T,
        "lnb": k["L0_conv_ln_b"].reshape(2, C).T,
        "woT": np.pad(k["L0_conv_out_proj_w"].T.reshape(2, C, C).transpose(1, 0, 2), ((0, 0), (0, 0), (0, 32))),
        "w1T": k["L1_conv_W1"].T,
        "w1n": k["L1_conv_W1"].reshape(3, 128, C).transpose(1, 0, 2),
        "b1": k["L1_conv_b1"].reshape(3, 128).T,
        "w2T": k["L1_conv_W2"].T.reshape(3, 128, C).transpose(1, 0, 2),
        "coef": k["L1_conv_coef"].reshape(3, 128, 3).transpose(1, 0, 2),
        "b2": k["L1_conv_b2"].reshape(1, C),
    }
    return {n: np.ascontiguousarray(v) for n, v in a.items()}


def kernel(**inputs):
    import concourse.bacc as _bacc
    from concourse.bass_utils import run_bass_kernel_spmd as _run

    data = lay_out(inputs)
    data.update(constants())
    nc = _bacc.Bacc("TRN2", target_bir_lowering=False, num_devices=1)
    arrays, S = {}, {}
    for name, a in data.items():
        arrays[f"in_{name}"] = a
        S[name] = nc.dram_tensor(f"in_{name}", a.shape, mybir.dt.from_np(a.dtype), kind="ExternalInput").ap()
    S["out"] = nc.dram_tensor("out_0_dram", (NB, HW, HW * C), F32, kind="ExternalOutput").ap()
    build_program(nc, S)
    r = _run(nc, [arrays], core_ids=[0])
    return np.asarray(r.results[0]["out_0_dram"]).reshape(NB, HW, HW, C)
```

```python
from contextlib import ExitStack

import numpy as np

import concourse.bass as bass
from concourse import mybir

ALU = mybir.AluOpType
ACT = mybir.ActivationFunctionType
AX = mybir.AxisListType
F32 = mybir.dt.float32
F32R = mybir.dt.float32r

NB = 8
HW = 64
L = HW * HW
C = 96
ND = 192
NS = 16
NK = 4
NR = 6
HID = 384
PADW = HW + 2
TC = 1024
NCH = L // TC
NG = 4
NJ = 3
YLAG = 4
HC2 = C // 2

FILL = ["x_pe", "x_ac", "x_ve", "dt_pe", "dt_ac0", "dt_ac1", "dt_ac2", "dt_ve", "dt_mul",
        "rep00_pe", "rep00_ac", "rep01_pe", "rep01_ac", "bc00_pe", "bc00_ac", "bc01_pe", "bc01_ac",
        "bc10_pe", "bc10_ac", "bc11_pe", "bc11_ac", "bc20_pe", "bc20_ac", "bc21_pe", "bc21_ac",
        "rep10_pe", "rep10_ac", "rep11_pe", "rep11_ac"]
NEW_CHUNK = [(0, "x_pe"), (2, "x_ac x_ve"), (3, "dt_pe rep01_pe dt_ac0 dt_ac1 dt_ac2"),
             (4, "dt_ve dt_mul rep00_pe"), (5, "rep00_ac rep01_ac"), (7, "bc00_pe bc11_pe bc00_ac"),
             (8, "bc01_pe bc10_pe"), (9, "bc01_ac bc11_ac bc10_ac rep11_pe rep10_pe"),
             (10, "bc20_pe rep11_ac bc21_pe rep10_ac"), (11, "bc20_ac bc21_ac"), (12, "rep21_pe rep20_pe"),
             (13, "rep21_ac rep20_ac"), (14, "rep31_pe"), (16, "rep31_ac"), (17, "rep30_pe"), (18, "rep30_ac")]
SAME_CHUNK = [(0, "dt_pe"), (1, "dt_ac0"), (2, "dt_ac1 dt_ac2"), (3, "dt_ve dt_mul"), (4, "bc00_pe"),
              (5, "bc00_ac"), (6, "bc10_pe"), (7, "bc11_pe"), (8, "bc01_pe"), (10, "bc11_ac bc01_ac bc20_pe"),
              (11, "bc20_ac bc21_pe"), (12, "bc21_ac bc10_ac")]
NEXT_IMAGE = [(7, "x_pe"), (8, "x_ac x_ve"), (9, "dt_pe"), (10, "dt_ac0 dt_ac1 dt_ac2"),
              (11, "dt_ve dt_mul bc00_pe bc01_pe bc00_ac bc01_ac rep00_pe rep01_pe rep00_ac rep01_ac"),
              (12, "bc10_pe bc11_pe bc10_ac bc11_ac"), (13, "bc20_pe bc21_pe bc20_ac bc21_ac"),
              (14, "rep10_pe rep11_pe rep10_ac rep11_ac"), (15, "rep20_pe rep21_pe"), (16, "rep20_ac rep21_ac"),
              (18, "rep30_pe rep31_pe"), (19, "rep30_ac rep31_ac")]
FIRST_CHUNK = [(4, "dt_pe"), (5, "dt_ac0 dt_ac1 dt_ac2 dt_ve dt_mul"), (8, "bc00_pe bc01_pe"),
               (9, "bc00_ac bc01_ac bc10_pe bc11_pe"), (10, "bc10_ac bc11_ac bc20_pe bc21_pe"), (11, "bc20_ac bc21_ac")]
CARRY_LAG = 2
UPLAG, BACKLAG = 1, 3
DLU_ON_VE = (0, 0, 0, 0)


class Queue:

    def __init__(self, sem):
        self.sem = sem
        self.n = 0
        self.items = []
        self.waited = {}

    def wait(self, *marks):
        for m in marks:
            if m is None:
                continue
            sem, count = m
            if self.waited.get(sem.num, 0) < count:
                self.waited[sem.num] = count
                self.items.append((0, sem, count))

    def op(self, fn, *marks):
        self.wait(*marks)
        self.n += 1
        self.items.append((1, fn, self.sem, 1))
        return (self.sem, self.n)

    def emit(self, eng):
        for it in self.items:
            if it[0] == 0:
                eng.wait_ge(it[1], it[2])
            elif it[0] == 2:
                eng.preload_act_table_set("natural_log_exp_and_others")
            else:
                it[1](eng).then_inc(it[2], it[3])


class DmaRing:

    def __init__(self, queue, sems):
        self.queue = queue
        self.sems = sems
        self.counts = [0] * len(sems)
        self.i = 0

    def dma(self, out, in_, *marks):
        k = self.i % len(self.sems)
        self.i += 1
        if self.counts[k]:
            self.queue.wait((self.sems[k], self.counts[k]))
        self.queue.wait(*marks)
        self.counts[k] += 16
        self.queue.items.append((1, lambda e: e.dma_start(out, in_), self.sems[k], 16))
        return (self.sems[k], self.counts[k])

    def drain(self):
        for s, c in zip(self.sems, self.counts):
            if c:
                self.queue.wait((s, c))


class Phase:

    def __init__(self, nc, ctx, name):
        def sem(x):
            return ctx.enter_context(nc.semaphore(f"{name}_{x}"))

        self.nc = nc
        self.pe, self.ve, self.ac, self.po, self.sp = (Queue(sem(x)) for x in ("pe", "ve", "ac", "po", "sp"))
        self.ld = DmaRing(self.sp, [sem(f"ld{i}") for i in range(6)])
        self.st = DmaRing(self.sp, [sem(f"st{i}") for i in range(6)])

    def run(self):
        self.ld.drain()
        self.st.drain()
        with self.nc.Block() as block:
            @block.sync
            def _(e):
                self.sp.emit(e)

            @block.tensor
            def _(e):
                self.pe.emit(e)

            @block.vector
            def _(e):
                self.ve.emit(e)

            @block.scalar
            def _(e):
                self.ac.emit(e)

            @block.gpsimd
            def _(e):
                self.po.emit(e)


def pre_phase(nc, P, T, S):
    win, cwr, cww, cb, gmat, eps = (T(n, s) for n, s in (
        ("win", [C, 2 * ND]), ("cwr", [C, 9, C]), ("cww", [C, 9]), ("cb", [C, 2]), ("gmat", [C, C]), ("eps", [C, 1])))
    wtap = [T(f"wtap{i}", [C, 9, C], F32R) for i in range(2)]
    wins = [T(f"wins{i}", [C, 2 * ND], F32R) for i in range(2)]
    m_w = [P.ld.dma(win[:], S["winT"]), P.ld.dma(cwr[:], S["cwr"]), P.ld.dma(cb[:], S["cb"]),
           P.ld.dma(cww[:], S["cww"]), P.ld.dma(gmat[:], S["gmat"])]
    m_eps = P.ve.op(lambda e: e.memset(eps[:], 1e-5))
    m = P.ve.op(lambda e: e.tensor_copy(wins[0][:], win[:]), *m_w)
    m = P.ve.op(lambda e: e.tensor_tensor(wins[1][:], win[:], wins[0][:], ALU.subtract), m)
    for t in range(9):
        m = P.ve.op(lambda e, t=t: e.tensor_tensor(cwr[:, t, :], win[:, 0:C], cwr[:, t, :], ALU.mult), *m_w)
    m = P.ve.op(lambda e: e.tensor_copy(wtap[0][:], cwr[:]), m)
    m_tap = P.ve.op(lambda e: e.tensor_tensor(wtap[1][:], cwr[:], wtap[0][:], ALU.subtract), m)

    xt = [T(f"xt{i}", [C, L]) for i in range(2)]
    xp = [[T(f"xp{i}{j}", [C, PADW, PADW], F32R) for j in range(2)] for i in range(2)]
    xc = [T(f"xc{i}", [C, PADW, PADW]) for i in range(2)]
    NX = 6
    xs = T("xs", [C, NX, 1024])
    st = T("st", [C, 8, 6])
    mv = T("mv", [C, 8])
    ps = S["psum"]
    m_pad = []
    for t in (xp[0][0], xp[0][1], xc[0], xp[1][0], xp[1][1], xc[1]):
        a = t[:].bitcast(F32) if t.dtype == F32R else t[:]
        m_pad += [P.po.op(lambda e, v=v: e.memset(v, 0.0)) for v in (a[:, 0, :], a[:, PADW - 1, :], a[:, 1:HW + 1, 0:1], a[:, 1:HW + 1, HW + 1:PADW])]
    ps_free = [None] * 8
    xs_free = [None] * NX
    free = {}
    count = [0, 0]
    late = []

    def bank():
        g = count[0] % 8
        count[0] += 1
        return g, ps_free[g]

    def slot():
        x = count[1] % NX
        count[1] += 1
        return x, xs_free[x]

    def store(x, name, b, half, q, m):
        xs_free[x] = P.st.dma(S[name][b, half, :, q * 1024:(q + 1) * 1024], xs[:, x, :], m)

    def load(b):
        s = b % 2
        free[("x", b)] = P.ld.dma(xt[s][:], S["xT"][b], free.get(("xt", s)))

    def stats(b):
        s = b % 2
        for i in range(8):
            m = P.ve.op(lambda e, i=i: e.bn_stats(st[:, i, :], xt[s][:, i * 512:(i + 1) * 512]), free[("x", b)])
        m = P.ve.op(lambda e: e.bn_aggr(mv[:, 0:2], st[:].rearrange("p a b -> p (a b)")), m, free.get("mv"))
        m = P.ve.op(lambda e: e.scalar_tensor_tensor(mv[:, 1:2], mv[:, 0:1], mv[:, 0:1], mv[:, 1:2], ALU.mult, ALU.add), m)
        g, fr = bank()
        m = P.pe.op(lambda e: e.matmul(ps[g][0:C, 0:2], gmat[:], mv[:, 0:2], start=True, stop=True), m, m_w[4], fr)
        m = ps_free[g] = P.ve.op(lambda e: e.tensor_copy(mv[:, 2:4], ps[g][0:C, 0:2]), m)
        m = P.ve.op(lambda e: e.scalar_tensor_tensor(mv[:, 4:5], mv[:, 2:3], mv[:, 2:3], mv[:, 3:4], ALU.mult, ALU.subtract), m)
        m = P.ac.op(lambda e: e.activation(mv[:, 5:6], mv[:, 4:5], ACT.Ln, bias=eps[:], scale=-1.0), m, m_eps)
        m = P.ac.op(lambda e: e.activation(mv[:, 6:7], mv[:, 5:6], ACT.Exp, scale=-0.5), m)
        free[("norm", b)] = P.ve.op(lambda e: e.scalar_tensor_tensor(mv[:, 7:8], mv[:, 2:3], -1.0, mv[:, 6:7], ALU.mult, ALU.mult), m)

    def normalise(b):
        s = b % 2
        v = xt[s][:].rearrange("p (h w) -> p h w", w=HW)
        m = free["mv"] = P.ac.op(lambda e: e.activation(xt[s][:], xt[s][:], ACT.Identity, bias=mv[:, 7:8], scale=mv[:, 6:7]),
                                 free[("norm", b)])
        hi, lo = (t[:, 1:HW + 1, 1:HW + 1] for t in xp[s])
        m = P.po.op(lambda e: e.tensor_copy(hi, v), m, free.get(("xp", s)), *m_pad)
        m = P.po.op(lambda e: e.tensor_tensor(lo, v, hi, ALU.subtract), m)
        free[("xt", s)] = free[("xn", b)] = m

    def product(o, w, x, first, last):
        def mm(e):
            for i, (p, q) in enumerate(((0, 0), (0, 1), (1, 0))):
                r = e.matmul(o, w[p], x[q], start=first and i == 0, stop=last and i == 2)
            return r
        return mm

    def project(b, col, h0, fn):
        s = b % 2
        g, fr = bank()
        m = P.pe.op(product(ps[g][0:C, :], [w[:, col:col + C] for w in wins],
                            [x[:, h0 + 1:h0 + 9, 1:HW + 1] for x in xp[s]], True, True), free[("xn", b)], m_tap, fr)
        ps_free[g] = m = fn(g, m)
        return m

    def inner(b):
        s = b % 2
        for r in range(8):
            to = xc[s][:, r * 8 + 1:r * 8 + 9, 1:HW + 1]
            free[("xc", b, r)] = project(b, C, r * 8, lambda g, m, to=to: P.ac.op(
                lambda e: e.copy(to, ps[g][0:C, :].rearrange("p (h w) -> p h w", w=HW)), m, free.get(("xc", s)), *m_pad))

    def conv_pe(b, q):
        s = b % 2
        x, fx = slot()
        for r in range(2):
            h0 = q * 16 + r * 8
            g, fr = bank()

            def mm(e, g=g, h0=h0):
                for t in range(9):
                    i = product(ps[g][0:C, :], [w[:, t, :] for w in wtap],
                                [v[:, h0 + t // 3:h0 + t // 3 + 8, t % 3:t % 3 + HW] for v in xp[s]], t == 0, t == 8)(e)
                return i
            m = P.pe.op(mm, free[("xn", b)], m_tap, fr)
            free[("xp", s)] = m
            m = ps_free[g] = P.ac.op(lambda e, g=g, r=r: e.activation(
                xs[:, x, r * 512:(r + 1) * 512], ps[g][0:C, :], ACT.Silu, bias=cb[:, 0:1]), m, fx, *m_w)
        store(x, "xa", b, 0, q, m)

    def gate(b, half, q):
        x, fx = slot()
        for r in range(2):
            m = project(b, ND + half * C, q * 16 + r * 8, lambda g, m, r=r: P.ac.op(
                lambda e: e.activation(xs[:, x, r * 512:(r + 1) * 512], ps[g][0:C, :], ACT.Silu), m, fx))
        free[("xp", b % 2)] = (P.pe.sem, P.pe.n)
        store(x, "sz", b, half, q, m)

    def conv_ve(b, q):
        s = b % 2
        x, fx = slot()
        acc = xs[:, x, :].rearrange("p (h w) -> p h w", w=HW)
        m = None
        for t in range(9):
            v = xc[s][:, q * 16 + t // 3:q * 16 + t // 3 + 16, t % 3:t % 3 + HW]
            if t == 0:
                m = P.ve.op(lambda e, v=v: e.tensor_scalar(acc, v, cww[:, 0:1], None, ALU.mult), fx,
                            free[("xc", b, min(7, 2 * q + 2))], *m_w)
            else:
                m = P.ve.op(lambda e, v=v, t=t: e.scalar_tensor_tensor(acc, v, cww[:, t:t + 1], acc, ALU.mult, ALU.add), m)
        free[("xc", s)] = m

        def silu():
            m2 = P.ac.op(lambda e: e.activation(xs[:, x, :], xs[:, x, :], ACT.Silu, bias=cb[:, 1:2]), m, *m_w)
            store(x, "xa", b, 1, q, m2)
        late.append(silu)

    load(0)
    if NB > 1:
        load(1)
    stats(0)
    normalise(0)
    for b in range(NB):
        inner(b)
        for q in range(4):
            conv_pe(b, q)
            if late:
                late.pop(0)()
            conv_ve(b, q)
            for half in range(2):
                gate(b, half, q)
            if q == 0 and b + 1 < NB:
                stats(b + 1)
            if q == 1 and b + 1 < NB:
                normalise(b + 1)
                if b + 2 < NB:
                    load(b + 2)
    late.pop(0)()
    P.run()


def scan_phase(nc, P, T, S):
    wx = T("wx", [C, NK, 2, C + NR])
    dtw = T("dtw", [C + NR, NK * ND])
    dtb = T("dtb", [C, NK * 2])
    ndtb = T("ndtb", [C, NK * 2])
    c20 = T("c20", [C, 1])
    am = T("am", [128, NK * 2 * NJ * NG])
    selb = T("selb", [C, 8, 128], F32R)
    seld = T("seld", [C, NJ, 128])
    sely = T("sely", [128, 32])
    rep = T("rep", [128, NG, 2, TC])
    selbf = rep[0:C, 0, 0, :].rearrange("p (a b) -> p a b", b=128)
    m_c = [P.ld.dma(wx[:], S["wx"]), P.ld.dma(dtw[C:C + NR, :], S["dtw"]), P.ld.dma(dtb[:], S["dtb"]),
           P.ld.dma(am[:], S["alog"]), P.ld.dma(selbf, S["selb"]),
           P.ld.dma(seld[:], S["seld"]), P.ld.dma(sely[:], S["sely"])]
    P.ac.items.append((2,))
    m = P.ac.op(lambda e: e.activation(am[:], am[:], ACT.Exp), *m_c)
    m_am = P.ac.op(lambda e: e.mul(am[:], am[:], -1.0), m)
    m_sel = P.ve.op(lambda e: e.tensor_copy(selb[:], selbf), *m_c)
    m_c20 = P.ve.op(lambda e: e.memset(c20[:], 20.0))
    m_nb = P.ve.op(lambda e: e.tensor_scalar(ndtb[:], dtb[:], -1.0, 20.0, ALU.mult, ALU.add))

    u = T("u", [C, 2, L])
    yt = T("yt", [C, TC])
    NRING = 6
    dlr = T("dlr", [128, NRING, TC])
    dur = T("dur", [128, NRING, TC])
    NE, NH, NC_, ND_ = 4, 3, 6, 3
    E = T("E", [128, NE, TC])
    H = T("H", [128, NH, TC])
    HC = T("HC", [128, NC_, TC])
    dlt = T("dlt", [C + NR, TC])
    dl, dts = dlt[0:C, :], dlt[C:C + NR, :]
    dlu = T("dlu", [C, TC])
    sx = T("sx", [C, TC], F32R)
    car = T("car", [128, 2 * NJ * NG])
    psum = S["psumall"]
    stage = [psum[:, 0:1024], psum[:, 1024:2048], psum[:, 2048:3072]]
    dbu = T("dbu", [128, ND_, TC])
    yps = psum[:, 3072:4096]

    free = {}
    stage_idle = [0, 1, 2]

    def view(t, k, half, t0):
        if k % 2 == 0:
            return t[:, half, t0:t0 + TC]
        return t[:, half, :].rearrange("p (h w) -> p w h", w=HW)[:, t0 // HW:(t0 + TC) // HW, :]

    def viewn(t, k, half, t0, n):
        if k % 2 == 0:
            return t[:, half, t0:t0 + n]
        return t[:, half, :].rearrange("p (h w) -> p w h", w=HW)[:, t0 // HW:(t0 + n) // HW, :]

    def shaped(ap, k):
        return ap if k % 2 == 0 else ap.rearrange("p (w h) -> p w h", h=HW)

    def next_stage():
        i = stage_idle.pop(0)
        return i, free.get(("stage", i))

    def stage_done(i, m):
        stage_idle.append(i)
        free[("stage", i)] = m

    steps = [(b, k, ci, half) for b in range(NB) for k in range(NK) for ci in range(NCH) for half in range(2)]
    m_u = {}
    rep_ready = {}
    rep_used = {(0, 0): m_sel}
    slots = {}
    u_reads = []

    def t_of(k, ci):
        return TC * (ci if k < 2 else NCH - 1 - ci)

    def load_u(b):
        m_u[b] = [P.ld.dma(u[:, h, :], S["xa"][b, h], *u_reads) for h in range(2)]

    def prep(n):
        b, k, ci, half = steps[n]
        t0 = t_of(k, ci)
        st = {}
        kk = k * 2 + half

        def x_pe():
            i, fr = next_stage()

            def mm(e):
                for sub in range(2):
                    for h in range(2):
                        r = e.matmul(stage[i][0:C + NR, sub * 512:(sub + 1) * 512], wx[:, k, h, :],
                                     viewn(u, k, h, t0 + sub * 512, 512), start=(h == 0), stop=(h == 1))
                return r
            st["x"] = i, P.pe.op(mm, fr, *m_u[b], *m_c)
            u_reads.append(st["x"][1])

        def x_ac():
            i, m = st["x"]
            st_x["dts"] = P.ac.op(lambda e: e.copy(dts, stage[i][C:C + NR, :]), m, free.get("dts"))
            st["sx"] = P.ac.op(lambda e: e.copy(sx[0:C, :], stage[i][0:C, :]), m, free.get("sx"))

        def x_ve():
            i, _ = st["x"]
            m = P.ve.op(lambda e: e.tensor_tensor(sx[64:96, :], stage[i][64:96, :], sx[64:96, :], ALU.subtract),
                        st["sx"], st_x["dts"])
            st_x["sx"] = m
            stage_done(i, m)

        def rep_pe(g, c):
            i, fr = next_stage()

            def mm(e):
                for sub in range(2):
                    r = e.matmul(stage[i][:, sub * 512:(sub + 1) * 512], selb[:, 2 * g + c, :],
                                 sx[0:C, sub * 512:(sub + 1) * 512], start=True, stop=True)
                return r
            free["sx"] = m = P.pe.op(mm, fr, st_x["sx"], m_sel)
            st[("rep", g, c)] = i, m

        def rep_ac(g, c):
            i, m = st[("rep", g, c)]
            rep_ready[(g, c)] = P.ac.op(lambda e: e.copy(rep[:, g, c, :], stage[i][:]), m, rep_used.get((g, c)))
            stage_done(i, rep_ready[(g, c)])

        def dt_pe():
            i, fr = next_stage()

            def mm(e):
                for sub in range(2):
                    r = e.matmul(stage[i][0:C, sub * 512:(sub + 1) * 512],
                                 dtw[C:C + NR, k * ND + half * C:k * ND + (half + 1) * C],
                                 dts[:, sub * 512:(sub + 1) * 512], start=True, stop=True)
                return r
            free["dts"] = m = P.pe.op(mm, fr, st_x["dts"], *m_c)
            st["dt"] = i, m

        def dt_ac0():
            i, m = st["dt"]
            st["relu"] = P.ac.op(lambda e: e.activation(dlu[:], stage[i][0:C, :], ACT.Relu, bias=ndtb[:, kk:kk + 1],
                                                        scale=-1.0), m, free.get("dlu"), m_nb)

        def dt_ac1():
            st["exp"] = P.ac.op(lambda e: e.activation(dlu[:], dlu[:], ACT.Exp, bias=c20[:], scale=-1.0),
                                st["relu"], m_c20)

        def dt_ac2():
            st["ln"] = P.ac.op(lambda e: e.activation(dlu[:], dlu[:], ACT.Ln, bias=1.0), st["exp"])

        def dt_ve():
            i, _ = st["dt"]
            m = P.ve.op(lambda e: e.scalar_tensor_tensor(dl[:], stage[i][0:C, :], dtb[:, kk:kk + 1], dlu[:],
                                                         ALU.add, ALU.max), st["ln"], free.get("dl"))
            st["dl"] = m
            stage_done(i, m)

        def dt_mul():
            q = P.ve if DLU_ON_VE[n % 4] else P.po
            st["dlu"] = q.op(lambda e: e.tensor_tensor(shaped(dlu[:], k), shaped(dl[:], k), view(u, k, half, t0),
                                                       ALU.mult), st["dl"], *m_u[b])
            u_reads.append(st["dlu"])

        def bc_pe(j, c):
            src, key = ((dl, "dl"), (dlu, "dlu"))[c]
            i, fr = next_stage()

            def mm(e):
                for sub in range(2):
                    x = e.matmul(stage[i][:, sub * 512:(sub + 1) * 512], seld[:, j, :],
                                 src[:, sub * 512:(sub + 1) * 512], start=True, stop=True)
                return x
            free[key] = m = P.pe.op(mm, fr, st[key])
            st[("bc", j, c)] = i, m

        def bc_ac(j, c):
            r = (NJ * n + j) % NRING
            dst, key = ((dlr, "dl"), (dur, "dlu"))[c]
            i, m = st[("bc", j, c)]
            slots[(n, j, key)] = ma = P.ac.op(lambda e: e.copy(dst[:, r, :], stage[i][:]), m, free.get((key, "ring", r)))
            stage_done(i, ma)

        fs = {"x_pe": x_pe, "x_ac": x_ac, "x_ve": x_ve, "dt_pe": dt_pe, "dt_ac0": dt_ac0, "dt_ac1": dt_ac1,
              "dt_ac2": dt_ac2, "dt_ve": dt_ve, "dt_mul": dt_mul}
        for c in range(2):
            for j in range(NJ):
                fs[f"bc{j}{c}_pe"] = lambda j=j, c=c: bc_pe(j, c)
                fs[f"bc{j}{c}_ac"] = lambda j=j, c=c: bc_ac(j, c)
            for g in range(NG):
                fs[f"rep{g}{c}_pe"] = lambda g=g, c=c: rep_pe(g, c)
                fs[f"rep{g}{c}_ac"] = lambda g=g, c=c: rep_ac(g, c)
        return fs

    st_x = {}

    def unit(n, g, j, un):
        b, k, ci, half = steps[n]
        r = (NJ * n + j) % NRING
        ae = ((k * 2 + half) * NJ + j) * NG + g
        e_ = un % NE
        m_e = P.ac.op(lambda e: e.activation(E[:, e_, :], dlr[:, r, :], ACT.Exp, scale=am[:, ae:ae + 1]),
                      slots[(n, j, "dl")], free.get(("E", e_)), m_am)
        if g == NG - 1:
            free[("dl", "ring", r)] = m_e
        d_ = un % ND_
        m_d = P.ve.op(lambda e: e.tensor_tensor(dbu[:, d_, :], dur[:, r, :], rep[:, g, 0, :], ALU.mult),
                      slots[(n, j, "dlu")], rep_ready[(g, 0)], free.get(("dbu", d_)))
        if g == NG - 1:
            free[("dlu", "ring", r)] = m_d
        rep_used[(g, 0)] = m_d
        if pending:
            pending.pop()()
        pending.append(lambda: unit_tail(n, g, j, un, m_e, m_d))

    def unit_tail(n, g, j, un, m_e, m_d):
        b, k, ci, half = steps[n]
        cc = (half * NJ + j) * NG + g
        e_, h_, c_, d_ = un % NE, un % NH, un % NC_, un % ND_
        init = 0.0 if ci == 0 else car[:, cc:cc + 1]
        if k < 2:
            def scan(e):
                return e.tensor_tensor_scan(H[:, h_, :], E[:, e_, :], dbu[:, d_, :], init, ALU.mult, ALU.add)
            last = TC - 1
        else:
            def scan(e):
                return e.tensor_tensor_scan(H[:, h_, ::-1], E[:, e_, ::-1], dbu[:, d_, ::-1], init, ALU.mult, ALU.add)
            last = 0
        m_h = P.ve.op(scan, m_d, m_e, free.get(("H", h_)), free.get(("Hcar", h_)), free.get(("car", cc)))
        free[("dbu", d_)] = m_h
        free[("E", e_)] = m_h
        m_p = P.po.op(lambda e: e.tensor_tensor(HC[:, c_, :], H[:, h_, :], rep[:, g, 1, :], ALU.mult),
                      m_h, rep_ready[(g, 1)], free.get(("HC", c_)))
        rep_used[(g, 1)] = m_p
        free[("H", h_)] = m_p

        def carry():
            free[("car", cc)] = free[("Hcar", h_)] = P.ac.op(
                lambda e: e.copy(car[:, cc:cc + 1], H[:, h_, last:last + 1]), m_h)
        if ci < NCH - 1:
            at(un + CARRY_LAG, carry)
        group.append((c_, j, m_p))
        if j == NJ - 1:
            items = list(group)
            group.clear()

            def mm(e):
                for sub in range(2):
                    for (c, jj, _) in items:
                        x = e.matmul(yps[32 * jj:32 * jj + 32, sub * 512:(sub + 1) * 512], sely[:],
                                     HC[:, c, sub * 512:(sub + 1) * 512], start=(g == 0), stop=(g == NG - 1))
                return x

            def ysum():
                m = P.pe.op(mm, m_p, free.get("yps") if g == 0 else None)
                for (c, _, _) in items:
                    free[("HC", c)] = m
                free["ydone"] = m
            at(un + YLAG, ysum)

    group = []
    pending = []
    events = {}

    def at(when, fn):
        events.setdefault(when, []).append(fn)

    def yout(n):
        b, k, ci, half = steps[n]
        t0 = t_of(k, ci)
        m = P.ac.op(lambda e: e.copy(yt[:], yps[0:C, :]), free["ydone"], free.get("yt"))
        free["yps"] = m
        free["yt"] = P.st.dma(S["yk"][b, k, half, :, t0:t0 + TC], yt[:], m)

    load_u(0)
    fs = prep(0)
    for name in FILL:
        fs[name]()
    for g in (2, 3):
        for c in range(2):
            at(6 * g - 12, fs[f"rep{g}{c}_pe"])
            at(6 * g - 11, fs[f"rep{g}{c}_ac"])
    un = 0
    for n, (b, k, ci, half) in enumerate(steps):
        at(un + 12 + YLAG, lambda n=n: yout(n))
        if n + 1 < len(steps):
            nb, _, _, nh = steps[n + 1]
            fs = prep(n + 1)
            if nb != b:
                u_done = list(u_reads)
                u_reads.clear()
                m_u[nb] = [P.ld.dma(u[:, h, :], S["xa"][nb, h], *u_done) for h in range(2)]
            plan = NEXT_IMAGE if nb != b else NEW_CHUNK if nh == 0 else FIRST_CHUNK if (k, ci) == (0, 0) else SAME_CHUNK
            for x, names in plan:
                for name in names.split():
                    at(un + x, fs[name])
        for x in range(12):
            unit(n, x // NJ, x % NJ, un)
            for f in events.pop(un, ()):
                f()
            un += 1
    pending.pop()()
    while events:
        for f in events.pop(min(events)):
            f()
    P.run()


def skewed(count, *stages):
    for t in range(count + len(stages) - 1):
        for s in reversed(range(len(stages))):
            if 0 <= t - s < count:
                stages[s](t - s)
        yield


def post_phase(nc, P, T, S):
    jm = T("jm", [C, C])
    lng = T("lng", [C, 2])
    lnb = T("lnb", [C, 2])
    eps = T("eps2", [128, 1])
    wo = T("wo", [C, 2, 128])
    w1t = T("w1t", [128, HID])
    b1 = T("b1", [128, 3])
    w2s = T("w2s", [128, 3, 128])
    co = T("co", [128, 3, 3])
    b2 = T("b2", [1, C])
    ut = T("ut", [128, 128])
    dn = T("dn", [128, 128])
    g2 = T("g2", [128, 128])
    one = T("one", [128, 64])
    ds = T("ds", [C, 2, NK])
    dsum = T("dsum", [C, 2])
    y = T("y", [128, 2, L])
    x1 = T("x1", [128, HW, C])
    t1 = T("t1", [128, 64 * 128])
    t2 = T("t2", [128, 128, C])
    tmp = T("tmp", [C, 2, 1024])
    sz = T("szt", [C, 2, 2, 512])
    sq = tmp[:, 0, :].rearrange("p (a l) -> p a l", a=2)
    rs = tmp[:, 1, :].rearrange("p (a l) -> p a l", a=2)
    xu = [T(f"xu{i}", [128, 2, 512], F32R) for i in range(2)]
    hs = T("hs", [128, 2, 3, 512])
    s12 = T("s12", [128, 2, 128])
    cm = T("cm", [128, 8])
    w1s = [T(f"w1s{i}", [128, 2, HID], F32R) for i in range(2)]
    w1f = T("w1f", [128, HID])
    b1p = T("b1p", [128, 2, 3])
    b1a = T("b1a", [128, 2, 3])
    cr = T("cr", [1, C])
    w2t = t2[:, 0:3, :]
    m_c = [P.ld.dma(a, S[n]) for a, n in ((jm[:], "jmat"), (lng[:], "lng"), (lnb[:], "lnb"), (wo[:], "woT"),
                                          (w1t[:], "w1T"), (b1[:], "b1"), (w2t, "w2T"),
                                          (co[:], "coef"), (b2[:], "b2"), (ut[0:64, :], "upT"), (ut[64:128, :], "upT"),
                                          (dn[:], "dnT"), (g2[:], "gmat2"), (ds[:], "ds"))]
    m_eps = P.ve.op(lambda e: e.memset(eps[:], 1e-5))
    m_pad = [P.po.op(lambda e: e.memset(t1[:, HC2 * 128:], 0.0)), P.po.op(lambda e: e.memset(s12[:], 0.0))]
    m_one = P.ve.op(lambda e: e.memset(one[:], 1.0))
    m_ds = P.ve.op(lambda e: e.tensor_reduce(dsum[:], ds[:], AX.X, ALU.add), *m_c)
    m = P.ve.op(lambda e: e.memset(w2s[:], 0.0))
    m_w2s = P.ve.op(lambda e: e.tensor_copy(w2s[:, :, 0:C], w2t), m)
    ps = S["psum"]
    ps_free = [None] * 8
    turn = [0]
    free = {}
    done = {}

    def bank():
        g = turn[0] % 8
        turn[0] += 1
        return g, ps_free[g]

    def matmuls(g, fr, calls, *marks):
        def mm(e):
            for (o, l, r, first, last) in calls:
                x = e.matmul(o, l, r, start=first, stop=last)
            return x
        return P.pe.op(mm, fr, *marks)

    g, fr = bank()
    m = matmuls(g, fr, [(ps[g][0:1, 0:C], co[:, i, 0:1], w2t[:, i, :], i == 0, i == 2) for i in range(3)], *m_c)
    free["t2"] = m_r = ps_free[g] = P.ve.op(lambda e: e.tensor_tensor(cr[:], ps[0][0:1, 0:C], b2[:], ALU.add), m, m_w2s)

    def parts(o, w, x, first=True, last=True):
        return [(o, w[p], x[q], first and i == 0, last and i == 2) for i, (p, q) in enumerate(((0, 0), (0, 1), (1, 0)))]

    def gather(b):
        p = b % 2
        lo, hi = 64 * p, 64 * p + 64
        xb = x1[lo:hi, :, :]
        m_x1 = P.ld.dma(xb.rearrange("p w c -> p (w c)"), S["xh"][b], free.get(("x1", p)))
        m_y = []
        st = {}
        m_0 = [P.ld.dma(y[0:C, h, :], S["yk"][b, 0, h], free.get("y")) for h in range(2)]
        terms = [(h, k, part) for k in (2, 0, 1, 3) for part in range(4) for h in range(2)]

        ring = t2[0:C, :, :].rearrange("p a c -> p (a c)").rearrange("p (n l) -> p n l", l=1024) if b == 0 else tmp
        nr = 12 if b == 0 else 2

        def load(n):
            h, k, part = terms[n]
            src = S["yk"][b, k, h] if k else S["xa"][b, h]
            old = (free.get("t2"),) if b == 0 else (free.get(("sq", "rs")[n % 2]),)
            st[n] = P.ld.dma(ring[:, n % nr, :], src[:, part * 1024:(part + 1) * 1024], st.get(("tmp", n % nr)), *old)

        def add(n):
            h, k, part = terms[n]
            w = ring[:, n % nr, :]
            if k % 2:
                v = y[0:C, h, :].rearrange("p (h w) -> p w h", w=HW)[:, part * 16:part * 16 + 16, :]
                w = w.rearrange("p (w h) -> p w h", h=HW)
            else:
                v = y[0:C, h, part * 1024:(part + 1) * 1024]
            before = st.get(("add", h), m_0[0])
            if k:
                m = (P.po if h else P.ve).op(lambda e: e.tensor_tensor(v, v, w, ALU.add), st[n], before, *m_0)
            else:
                m = P.ve.op(lambda e: e.scalar_tensor_tensor(v, w, dsum[:, h:h + 1], v, ALU.mult, ALU.add),
                            st[n], before, m_ds, *m_0)
            st[("tmp", n % nr)] = st[("add", h)] = m
            if b == 0:
                free[("t2x", h)] = m

        for n in range(nr - 1):
            load(n)
        for n in range(len(terms)):
            if n + nr - 1 < len(terms):
                load(n + nr - 1)
            add(n)
            yield
        m_sum = (st[("add", 0)], st[("add", 1)])

        def mean(q):
            sl = slice(q * 512, (q + 1) * 512)
            st[("z", q)] = [P.ld.dma(sz[:, q % 2, h, :], S["sz"][b, h, :, sl], free.get(("sz", q % 2))) for h in range(2)]
            g, fr = bank()
            m = matmuls(g, fr, [(ps[g][0:C, :], jm[:], y[0:C, h, sl], h == 0, h == 1) for h in range(2)], *m_sum, *m_c)
            for h in range(2):
                m = P.ve.op(lambda e, h=h: e.tensor_tensor(y[0:C, h, sl], y[0:C, h, sl], ps[g][0:C, :], ALU.subtract), m)
            ps_free[g] = m
            st[("sq", q)] = P.ac.op(lambda e: e.activation(sq[:], y[0:C, :, sl], ACT.Square), m, free.get("sq"))
            st[("yc", q)] = m

        def var(q):
            g, fr = bank()
            free["sq"] = m = matmuls(g, fr, [(ps[g][0:C, :], jm[:], sq[:, h, :], h == 0, h == 1) for h in range(2)],
                                     st[("sq", q)])
            s = q % 2
            m = ps_free[g] = P.ac.op(lambda e: e.activation(rs[:, s, :], ps[g][0:C, :], ACT.Ln, bias=eps[0:C, :]), m, m_eps,
                                     free.get(("rs", s)))
            st[("rs", q)] = P.ac.op(lambda e: e.activation(rs[:, s, :], rs[:, s, :], ACT.Exp, scale=-0.5), m)

        def scale(q):
            sl = slice(q * 512, (q + 1) * 512)
            s = q % 2
            for h in range(2):
                m = P.ve.op(lambda e, h=h: e.tensor_tensor(y[0:C, h, sl], y[0:C, h, sl], rs[:, s, :], ALU.mult), st[("rs", q)])
            free[("rs", s)] = free["rs"] = m
            for h in range(2):
                m2 = P.ac.op(lambda e, h=h: e.activation(y[0:C, h, sl], y[0:C, h, sl], ACT.Identity,
                                                         bias=lnb[:, h:h + 1], scale=lng[:, h:h + 1]), m, *m_c)
            for h in range(2):
                m = P.po.op(lambda e, h=h: e.tensor_tensor(y[0:C, h, sl], y[0:C, h, sl], sz[:, s, h, :], ALU.mult),
                            m2, *st[("z", q)])
            free[("sz", s)] = st["y2"] = m

        yield from skewed(8, mean, var, scale)
        yv = y[0:C, :, :].rearrange("p a (h w) -> p a w h", w=HW)

        def project(n):
            w0 = 4 * n
            g, fr = bank()
            m = free["y"] = matmuls(g, fr, [(ps[g][lo:hi, w * 128:(w + 1) * 128], yv[:, h, w0 + w, :], wo[:, h, :], h == 0, h == 1)
                                            for w in range(4) for h in range(2)], st["y2"])
            st["x"] = ps_free[g] = P.ve.op(lambda e: e.tensor_tensor(
                xb[:, w0:w0 + 4, :], xb[:, w0:w0 + 4, :],
                ps[g][lo:hi, :].rearrange("p (w c) -> p w c", c=128)[:, :, 0:C], ALU.add), m, m_x1)

        yield from skewed(16, project)
        m_x = done[("x", b)] = st["x"]
        yf = y[lo:hi, :, :].rearrange("p a l -> p (a l)")[:, 0:HW * C]
        xsq = yf.rearrange("p (w c) -> p w c", c=C)
        ma = None
        for i in range(4):
            ma = P.ac.op(lambda e, i=i: e.activation(xsq[:, 16 * i:16 * i + 16, :], xb[:, 16 * i:16 * i + 16, :], ACT.Square),
                         m_x, free["y"])
            yield
        for c0, o in ((0, 0), (HC2, 64)):
            m1 = P.ve.op(lambda e, c0=c0, o=o: e.tensor_reduce(
                s12[lo:hi, 0, o:o + HC2], xb.rearrange("p w c -> p c w")[:, c0:c0 + HC2, :], AX.X, ALU.add), m_x,
                free.get("s12"), *m_pad)
            yield
        for c0, o in ((0, 0), (HC2, 64)):
            m2 = P.ve.op(lambda e, c0=c0, o=o: e.tensor_reduce(
                s12[lo:hi, 1, o:o + HC2], xsq.rearrange("p w c -> p c w")[:, c0:c0 + HC2, :], AX.X, ALU.add), ma)
            yield
        free["y"] = m2
        g, fr = bank()
        m = free["s12"] = matmuls(g, fr, [(ps[g][:, i:i + 1], s12[lo:hi, i, :], one[lo:hi, 0:1], True, True) for i in range(2)],
                                  m1, m2, m_one)
        m = ps_free[g] = P.ve.op(lambda e, g=g: e.tensor_copy(cm[:, 0:2], ps[g][:, 0:2]), m, free.get("cm"))
        g, fr = bank()
        m = matmuls(g, fr, [(ps[g][:, 0:2], g2[:], cm[:, 0:2], True, True)], m)
        m = ps_free[g] = P.ve.op(lambda e, g=g: e.tensor_copy(cm[:, 2:4], ps[g][:, 0:2]), m)
        m = P.ve.op(lambda e: e.scalar_tensor_tensor(cm[:, 4:5], cm[:, 2:3], cm[:, 2:3], cm[:, 3:4], ALU.mult, ALU.subtract), m)
        yield
        m = P.ac.op(lambda e: e.activation(cm[:, 5:6], cm[:, 4:5], ACT.Ln, bias=eps[:], scale=-1.0), m)
        m = P.ac.op(lambda e: e.activation(cm[:, 6:7], cm[:, 5:6], ACT.Exp, scale=-0.5), m)
        yield
        m = P.ve.op(lambda e: e.scalar_tensor_tensor(cm[:, 7:8], cm[:, 2:3], -1.0, cm[:, 6:7], ALU.mult, ALU.mult), m)
        m_w = P.ve.op(lambda e: e.tensor_scalar(w1f[:], w1t[:], cm[:, 6:7], None, ALU.mult), m)
        m_w = P.ve.op(lambda e: e.tensor_copy(w1s[0][:, p, :], w1f[:]), m_w, free.get(("w1s", p)))
        m_w = P.ve.op(lambda e: e.tensor_tensor(w1s[1][:, p, :], w1f[:], w1s[0][:, p, :], ALU.subtract), m_w)
        yield
        g, fr = bank()
        m = free["cm"] = matmuls(g, fr, [(ps[g][:, i:i + 1], w1t[:, i * 128:(i + 1) * 128], cm[:, 7:8], True, True)
                                         for i in range(3)], m)
        m = ps_free[g] = P.ve.op(lambda e, g=g: e.tensor_tensor(b1p[:, p, :], ps[g][:, 0:3], b1[:], ALU.add), m,
                                 free.get(("b1p", p)))
        m = P.ve.op(lambda e: e.tensor_tensor(b1a[:, p, :], b1p[:, p, :], co[:, :, 2], ALU.mult), m)
        m = P.ve.op(lambda e: e.tensor_tensor(b1a[:, p, :], b1a[:, p, :], co[:, :, 1], ALU.add), m)
        done[("scaled", b)] = (m_w, m)
        yield

    def resample(b):
        p = b % 2
        lo, hi = 64 * p, 64 * p + 64
        xb = x1[lo:hi, :, :]
        m_x = done[("x", b)]
        st = {"t1": {}}

        def up_h(n):
            c0 = 4 * n
            g, fr = bank()
            m = matmuls(g, fr, [(ps[g][o:o + 64, i * 128:(i + 1) * 128], xb[:, :, c0 + i + c], ut[lo:hi, :], True, True)
                                for i in range(4) for o, c in ((0, 0), (64, HC2))], m_x)
            to = t1[:, c0 * 128:(c0 + 4) * 128]
            if n % 2:
                m = P.ac.op(lambda e: e.copy(to, ps[g][:]), m, free.get("t1"))
            else:
                m = P.ve.op(lambda e: e.tensor_copy(to, ps[g][:]), m, free.get("t1"))
            ps_free[g] = st["t1"][n % 2] = m

        yield from skewed(12, up_h)
        m_w, m_b = done[("scaled", b)]
        t1v = t1[:, :].rearrange("p (c h) -> p c h", h=128)

        def up_w(q):
            h0, s = 4 * q, q % 2
            g, fr = bank()
            m = free["t1"] = matmuls(g, fr, [(ps[g][o:o + 64, i * 128:(i + 1) * 128], t1v[o:o + 64, :, h0 + i], ut[o:o + 64, :],
                                              True, True) for i in range(4) for o in (0, 64)], *st["t1"].values(), *m_pad)
            m = P.ac.op(lambda e: e.copy(xu[0][:, s, :], ps[g][:]), m, free.get(("xu", s)))
            st[("xu", q)] = ps_free[g] = P.ve.op(lambda e: e.tensor_tensor(xu[1][:, s, :], ps[g][:], xu[0][:, s, :],
                                                                           ALU.subtract), m)

        def hidden(q):
            s = q % 2
            for i in range(3):
                g, fr = bank()
                m = free[("w1s", p)] = free[("xu", s)] = matmuls(
                    g, fr, parts(ps[g][:], [w[:, p, i * 128:(i + 1) * 128] for w in w1s], [x[:, s, :] for x in xu]),
                    st[("xu", q)], m_w)
                m = P.ac.op(lambda e, g=g, i=i: e.activation(hs[:, s, i, :], ps[g][:], ACT.Identity, bias=b1a[:, p, i:i + 1],
                                                             scale=co[:, i, 2:3]), m, m_b, free.get(("hs", s)))
                m = ps_free[g] = P.ve.op(lambda e, g=g, i=i: e.scalar_tensor_tensor(
                    hs[:, s, i, :], ps[g][:], b1p[:, p, i:i + 1], hs[:, s, i, :], ALU.add, ALU.mult), m)
            free[("b1p", p)] = st[("hs", q)] = m

        def back(q):
            s = q % 2
            g, fr = bank()
            m = free[("hs", s)] = matmuls(
                g, fr, [(ps[g][:, i * 128:(i + 1) * 128], hs[:, s, j, i * 128:(i + 1) * 128], w2s[:, j, :], j == 0, j == 2)
                        for i in range(4) for j in range(3)], st[("hs", q)], m_w2s)
            st["t2"] = ps_free[g] = P.ve.op(lambda e: e.tensor_copy(
                t2[:, 4 * q:4 * q + 4, :], ps[g][:].rearrange("p (h c) -> p h c", c=128)[:, :, 0:C]), m, free.get("t2"),
                    free[("t2x", 0)], free[("t2x", 1)])

        for q in range(32 + BACKLAG):
            if q < 32:
                up_w(q)
            if q >= BACKLAG:
                back(q - BACKLAG)
            if q >= UPLAG and q - UPLAG < 32:
                hidden(q - UPLAG)
            yield
        t3 = t1[:, 0:C * 64]

        def down_w(n):
            g, fr = bank()
            m = free["t2"] = matmuls(g, fr, [(ps[g][:, i * 128:(i + 1) * 128], t2[:, :, 4 * n + i], dn[:], True, True)
                                             for i in range(4)], st["t2"])
            st[("t3", n)] = ps_free[g] = P.ac.op(lambda e: e.copy(
                t3[:, n * 256:(n + 1) * 256].rearrange("p (c w) -> p c w", w=64),
                ps[g][:].rearrange("p (c w) -> p c w", w=128)[:, :, 0:64]), m, free["t1"])

        def down_h(n):
            if n % 2 == 0:
                return
            c0 = 4 * n - 4
            g, fr = bank()
            m = matmuls(g, fr, [(ps[g][lo:hi, :], dn[:, 0:64], t3[:, c0 * 64:(c0 + 8) * 64], True, False),
                                (ps[g][lo:hi, :], one[0:1, :], cr[0:1, c0:c0 + 8].unsqueeze(2).to_broadcast([1, 8, 64]),
                                 False, True)], st[("t3", n)], st[("t3", n - 1)], m_r)
            st["pe"] = m
            xc = xb[:, :, c0:c0 + 8].rearrange("p w c -> p c w")
            st["out"] = ps_free[g] = P.ve.op(lambda e: e.tensor_tensor(
                xc, xc, ps[g][lo:hi, :].rearrange("p (c w) -> p c w", w=64), ALU.add), m)

        yield from skewed(24, down_w, down_h)
        free["t1"] = st["pe"]
        free[("x1", p)] = P.st.dma(S["out"][b], xb.rearrange("p w c -> p (w c)"), st["out"])

    side = gather(0)
    while ("x", 0) not in done:
        next(side)
    for b in range(NB):
        for n, _ in enumerate(resample(b)):
            if n == 11:
                for _ in side:
                    pass
            if n == 12:
                side = gather(b + 1) if b + 1 < NB else iter(())
            for _ in range(1 + (n < 24)):
                next(side, None)
    for _ in side:
        pass
    P.run()


def build_program(nc, S):
    with ExitStack() as top:
        psum = top.enter_context(nc.psum_tensor("psum", [128, 4096], F32))
        S["psumall"] = psum
        S["psum"] = [psum[:, i * 512:(i + 1) * 512] for i in range(8)]
        for name, shape in (("xa", [NB, 2, C, L]), ("sz", [NB, 2, C, L]), ("yk", [NB, NK, 2, C, L])):
            S[name] = nc.dram_tensor(f"scr_{name}", shape, F32, kind="Internal").ap()
        for name, phase in (("pre", pre_phase), ("scan", scan_phase), ("post", post_phase)):
            with ExitStack() as ctx:
                def T(n, shape, dt=F32):
                    return ctx.enter_context(nc.sbuf_tensor(n, shape, dt))
                phase(nc, Phase(nc, ctx, name), T, S)


def halves(a):
    r = np.zeros((128,) + a.shape[1:], a.dtype)
    r[0:HC2], r[64:64 + HC2] = a[0:HC2], a[HC2:]
    return r


def constants():
    f = np.float32
    group = np.kron(np.eye(32), np.ones((3, 3)))
    ni, d = np.meshgrid(np.arange(4), np.arange(32), indexing="ij")
    p = (ni * 32 + d).ravel()
    selb = np.zeros((C, 8, 128), f)
    for g in range(4):
        for c in range(2):
            src = c * 16 + g * 4 + ni.ravel()
            selb[src, 2 * g + c, p] = 1
            selb[64 + src, 2 * g + c, p] = 1
    seld = np.zeros((C, 3, 128), f)
    for j in range(3):
        seld[32 * j + d.ravel(), j, p] = 1
    sely = np.zeros((128, 32), f)
    sely[p, d.ravel()] = 1

    def mask(edge):
        r = np.ones(128)
        r[33:96] = 0
        r[32] = r[96] = edge
        return r

    def operator(edge):
        return np.real(np.fft.ifft(np.fft.fft(np.eye(128), axis=0) * mask(edge)[:, None], axis=0))
    up = 2 * operator(1.0)[:, ::2]
    dn = operator(0.5)[::2, :]
    return {"gmat": (group / 3).astype(f), "gmat2": halves(halves((group / (3 * L)).astype(f)).T),
            "jmat": np.full((C, C), 1 / ND, f), "selb": selb, "seld": seld, "sely": sely,
            "upT": np.ascontiguousarray(up.T).astype(f),
            "dnT": np.concatenate([dn.T, np.zeros((128, 64))], axis=1).astype(f)}


def lay_out(i):
    k = {n: np.asarray(v) for n, v in i.items()}
    x = k["x"]
    wi = k["L0_conv_in_proj_w"]
    xp = k["L0_conv_x_proj_w"]
    wx = np.zeros((NK, C + NR, ND), np.float32)
    wx[:, 0:32] = xp[:, 6:38]
    wx[:, C:] = xp[:, 0:6]
    wx[:, 64:96] = xp[:, 6:38]
    a = {
        "xT": x.reshape(NB, L, C).transpose(0, 2, 1),
        "xh": x.reshape(NB, HW, HW * C),
        "winT": wi.T,
        "cwr": np.broadcast_to(k["L0_conv_conv_w"].reshape(ND, 9)[0:C].T[None], (C, 9, C)),
        "cww": k["L0_conv_conv_w"].reshape(ND, 9)[C:],
        "cb": k["L0_conv_conv_b"].reshape(2, C).T,
        "wx": wx.reshape(NK, C + NR, 2, C).transpose(3, 0, 2, 1),
        "dtw": k["L0_conv_dt_proj_w"].transpose(2, 0, 1).reshape(NR, NK * ND),
        "dtb": k["L0_conv_dt_proj_b"].reshape(NK, 2, C).transpose(2, 0, 1).reshape(C, NK * 2),
        "ds": k["L0_conv_Ds"].reshape(NK, 2, C).transpose(2, 1, 0),
        "alog": k["L0_conv_A_logs"].reshape(NK, 2, NJ, 32, NG, 4).transpose(5, 3, 0, 1, 2, 4).reshape(128, -1),
        "lng": k["L0_conv_ln_g"].reshape(2, C).T,
        "lnb": k["L0_conv_ln_b"].reshape(2, C).T,
        "woT": np.pad(k["L0_conv_out_proj_w"].T.reshape(2, C, C).transpose(1, 0, 2), ((0, 0), (0, 0), (0, 32))),
        "w1T": halves(k["L1_conv_W1"].T),
        "b1": k["L1_conv_b1"].reshape(3, 128).T,
        "w2T": k["L1_conv_W2"].T.reshape(3, 128, C).transpose(1, 0, 2),
        "coef": k["L1_conv_coef"].reshape(3, 128, 3).transpose(1, 0, 2),
        "b2": k["L1_conv_b2"].reshape(1, C),
    }
    return {n: np.ascontiguousarray(v) for n, v in a.items()}


def kernel(**inputs):
    import concourse.bacc as _bacc
    from concourse.bass_utils import run_bass_kernel_spmd as _run

    data = lay_out(inputs)
    data.update(constants())
    nc = _bacc.Bacc("TRN2", target_bir_lowering=False, num_devices=1)
    arrays, S = {}, {}
    for name, a in data.items():
        arrays[f"in_{name}"] = a
        S[name] = nc.dram_tensor(f"in_{name}", a.shape, mybir.dt.from_np(a.dtype), kind="ExternalInput").ap()
    S["out"] = nc.dram_tensor("out_0_dram", (NB, HW, HW * C), F32, kind="ExternalOutput").ap()
    build_program(nc, S)
    r = _run(nc, [arrays], core_ids=[0])
    return np.asarray(r.results[0]["out_0_dram"]).reshape(NB, HW, HW, C)
```
